# Optimizing a Trainium2 kernel written in Bass

```python
import numpy as np
import jax
import jax.numpy as jnp

def _softmax(x, axis=-1):
    return jax.nn.softmax(x, axis=axis)

def _gelu(x):
    return jax.nn.gelu(x, approximate=True)

def _silu(x):
    return jax.nn.silu(x)

def _sigmoid(x):
    return jax.nn.sigmoid(x)

def _layernorm(x, axis=-1, eps=1e-05):
    m = jnp.mean(x, axis=axis, keepdims=True)
    v = jnp.var(x, axis=axis, keepdims=True)
    return (x - m) / jnp.sqrt(v + eps)

def _scatter_add(tgt, idx, src, axis=0):
    return tgt.at[idx].add(src)

def _segment_sum(src, seg, n):
    return jax.ops.segment_sum(src, seg, n)
kernel_name = 'mk_adj_ffn_d1_adj_r2_02df37'

def setup_inputs(seed: int=0):
    np.random.seed(seed)
    _w = jnp.asarray

    def _rec_inputs():
        import jax
        import jax.numpy as jnp
        _gk = jax.random.key(seed)
        x = -0.0002928 + 1 * jax.random.normal(jax.random.fold_in(_gk, 1), (128, 128, 256), jnp.float32)
        _a = jax.random.bernoulli(jax.random.fold_in(_gk, 2), 0.03125, (128, 128, 128))
        _a = jnp.logical_or(_a, jnp.swapaxes(_a, -1, -2))
        _a = jnp.logical_or(_a, jnp.eye(128, dtype=bool))
        _af = _a.astype(jnp.float32)
        _af = _af * jax.random.uniform(jax.random.fold_in(_gk, 3), (128, 128, 128), jnp.float32, 0.05, 1)
        adj = _af
        return (x, adj)
    x, adj = _rec_inputs()

    def _L0_gnn_setup():
        import jax, jax.numpy as jnp
        import numpy as np
        B, N, DIN, DOUT, K = (4, 1024, 256, 256, 3)
        key = jax.random.key(seed)
        ks = jax.random.split(key, 8)
        X = jax.random.normal(ks[0], (B, N, DIN), dtype=jnp.float32)
        A = jax.random.uniform(ks[1], (B, N, N), dtype=jnp.float32)
        Wv = jax.random.normal(ks[2], (DIN, DOUT), dtype=jnp.float32) * 0.02
        bv = jax.random.normal(ks[3], (DOUT,), dtype=jnp.float32) * 0.02
        aw = jax.random.normal(ks[4], (2 * DOUT, 1), dtype=jnp.float32) * 0.05
        ab = jax.random.normal(ks[5], (1,), dtype=jnp.float32) * 0.05
        Wk = jax.random.normal(ks[6], (K, DIN, DOUT), dtype=jnp.float32) * 0.02
        bk = jax.random.normal(ks[7], (K, DOUT), dtype=jnp.float32) * 0.02
        return {'X': X, 'A': A, 'Wv': Wv, 'bv': bv, 'aw': aw, 'ab': ab, 'Wk': Wk, 'bk': bk}
    _L0_gnn_all = _L0_gnn_setup()
    _L0_gnn_in = {k: v for k, v in _L0_gnn_all.items() if k in ('Wv', 'bv', 'aw', 'ab', 'Wk', 'bk')}
    del _L0_gnn_all

    def _L0_ffn_setup():
        import jax, jax.numpy as jnp
        import numpy as np
        CAPACITY_FACTOR = 1.2
        key = jax.random.key(seed)
        k1, k2, k3 = jax.random.split(key, 3)
        B, S, D, E = (8, 2048, 256, 16)
        x = jax.random.normal(k1, (B, S, D), dtype=jnp.float32)
        switch_w = jax.random.normal(k2, (E, D), dtype=jnp.float32) * 0.02
        switch_b = jnp.zeros((E,), dtype=jnp.float32)
        expert_w = jax.random.normal(k3, (E, D, D), dtype=jnp.float32) * 0.02
        expert_b = jnp.zeros((E, D), dtype=jnp.float32)
        return {'x': x, 'switch_w': switch_w, 'switch_b': switch_b, 'expert_w': expert_w, 'expert_b': expert_b}
    _L0_ffn_all = _L0_ffn_setup()
    _L0_ffn_in = {k: v for k, v in _L0_ffn_all.items() if k in ('switch_w', 'switch_b', 'expert_w', 'expert_b')}
    del _L0_ffn_all
    return {'x': x, 'adj': adj, 'L0_gnn_Wv': _L0_gnn_in['Wv'], 'L0_gnn_bv': _L0_gnn_in['bv'], 'L0_gnn_aw': _L0_gnn_in['aw'], 'L0_gnn_ab': _L0_gnn_in['ab'], 'L0_gnn_Wk': _L0_gnn_in['Wk'], 'L0_gnn_bk': _L0_gnn_in['bk'], 'L0_ffn_switch_w': _L0_ffn_in['switch_w'], 'L0_ffn_switch_b': _L0_ffn_in['switch_b'], 'L0_ffn_expert_w': _L0_ffn_in['expert_w'], 'L0_ffn_expert_b': _L0_ffn_in['expert_b']}

def reference(x, adj, L0_gnn_Wv, L0_gnn_bv, L0_gnn_aw, L0_gnn_ab, L0_gnn_Wk, L0_gnn_bk, L0_ffn_switch_w, L0_ffn_switch_b, L0_ffn_expert_w, L0_ffn_expert_b):
    import jax
    import jax.numpy as jnp

    def _L0_gnn_ref(X, A, Wv, bv, aw, ab, Wk, bk):
        import jax, jax.numpy as jnp
        import numpy as np
        B, N, DIN, DOUT, K = (4, 1024, 256, 256, 3)
        d = Wv.shape[1]
        Xw = X @ Wv + bv
        sj = Xw @ aw[:d, 0]
        si = Xw @ aw[d:, 0]
        e = jax.nn.leaky_relu(sj[:, None, :] + si[:, :, None] + ab[0], negative_slope=0.2)
        alpha_matrix = A * jnp.exp(e)
        transition = alpha_matrix / (jnp.sum(alpha_matrix, axis=-1, keepdims=True) + 1e-12)
        H = jnp.zeros(X.shape[:-1] + (d,), dtype=X.dtype)
        Xk = X
        for k in range(Wk.shape[0]):
            H = H + Xk @ Wk[k] + bk[k]
            Xk = jnp.einsum('bij,bjd->bid', transition, Xk)
        return jax.nn.relu(H)

    def _L0_ffn_ref(x, switch_w, switch_b, expert_w, expert_b):
        import jax, jax.numpy as jnp
        import numpy as np
        CAPACITY_FACTOR = 1.2
        B, S, D = x.shape
        E = switch_w.shape[0]
        N = B * S
        xf = x.reshape(N, D)
        logits = xf @ switch_w.T + switch_b
        probs = jax.nn.softmax(logits, axis=-1)
        route_probs = jnp.max(probs, axis=-1)
        routes = jnp.argmax(probs, axis=-1)
        oh = jax.nn.one_hot(routes, E, dtype=jnp.int32)
        pos = jnp.take_along_axis(jnp.cumsum(oh, axis=0), routes[:, None], axis=1)[:, 0] - 1
        capacity = int(CAPACITY_FACTOR * N / E)
        keep = pos < capacity
        buf = jnp.zeros((E, capacity, D), dtype=xf.dtype).at[routes, pos].set(xf)
        y = jnp.einsum('ecd,efd->ecf', buf, expert_w) + expert_b[:, None, :]
        gathered = y[routes, jnp.minimum(pos, capacity - 1)]
        out = jnp.where(keep[:, None], gathered, xf) * route_probs[:, None]
        return out.reshape(B, S, D)
    x = x + _L0_gnn_ref(_layernorm(x, axis=-1), adj, L0_gnn_Wv, L0_gnn_bv, L0_gnn_aw, L0_gnn_ab, L0_gnn_Wk, L0_gnn_bk)
    x = x + _L0_ffn_ref(_layernorm(x, axis=-1), L0_ffn_switch_w, L0_ffn_switch_b, L0_ffn_expert_w, L0_ffn_expert_b)
    return x

_drawn_inputs = setup_inputs


def setup_inputs(seed=0):
    import zlib

    import numpy as np

    out = dict(_drawn_inputs(seed))
    spreads = {'L0_ffn_switch_b': (0.0, 0.1), 'L0_ffn_expert_b': (0.0, 0.772)}
    factors = {'L0_gnn_Wv': 3.259, 'L0_gnn_bv': 8.0, 'L0_gnn_aw': 3.327}
    for name, (base, spread) in spreads.items():
        noise = np.random.default_rng([zlib.crc32(name.encode()), seed]).standard_normal(out[name].shape)
        drawn = base * np.exp(spread * noise) if base else spread * noise
        out[name] = jnp.asarray(drawn.astype(out[name].dtype))
    for name, factor in factors.items():
        out[name] = (out[name] * factor).astype(out[name].dtype)
    return out
```

```python
from contextlib import ExitStack

import concourse.bass as bass
from concourse import mybir

P = 128
ALU = mybir.AluOpType
ACT = mybir.ActivationFunctionType
F32 = mybir.dt.float32
F32R = mybir.dt.float32r
BF16 = mybir.dt.bfloat16
U32 = mybir.dt.uint32
AX_X = mybir.AxisListType.X

EPS = 1e-5
ROW_EPS = 1e-12
SLOPE = 0.2
CAPACITY_FACTOR = 1.2
BODY = 16
G = 4
NOWHERE = 1.0e6

LAG_X1 = 2
LAG_XFT = 3
LAG_ROUTE = 7
LAG_OUT = 9
LEAD_STATS = 7
LEAD_X0 = 2
LEAD_XT = 1


def graph_then_experts(nc, x, adj, WvT, bv, aw, ab, Wk, bk, swT, sb_, ewT, eb, out):
    B, N, D = x.shape
    KT = D // P
    E = swT.shape[1]
    TOK = B * N
    CAP = int(CAPACITY_FACTOR * TOK / E)
    TPE = -(-CAP // P)
    REG = TPE * P
    HALF = TPE // 2
    ROW = D + 4
    NMR, RSTD, PROB, TOKEN = D, D + 1, D + 2, D + 3
    NV = 4
    W0C = D + NV
    PASSES = B // BODY
    EWR = 4
    NB = BODY // G
    assert N == P and TPE % 2 == 0 and Wk.shape[0] == 3 and B % BODY == 0

    rowbuf = nc.dram_tensor("rowbuf", [E * REG, ROW], F32, kind="Internal").ap()

    with ExitStack() as ctx:
        def sb(name, shape, dt=F32):
            return ctx.enter_context(nc.sbuf_tensor(name, shape, dt))

        def psum(name):
            return ctx.enter_context(nc.psum_tensor(name, [P, 512], F32))

        def sem(name):
            return ctx.enter_context(nc.semaphore(name))

        ps_z0 = [psum("ps_z0a"), psum("ps_z0b")]
        ps_z12 = [psum("ps_z12a"), psum("ps_z12b")]
        ps_xt = psum("ps_xt")
        ps_t = psum("ps_t")
        ps_lg = psum("ps_lg")
        ps_set = psum("ps_set")

        ident = sb("ident", [P, P])
        onesf = sb("onesf", [P, P])
        steps_bf = sb("steps_bf", [P, P], BF16)
        before_bf = sb("before_bf", [P, P], BF16)
        ones2 = sb("ones2", [2, P], F32R)
        rev = sb("rev", [P, G, E])
        swb = sb("swb", [P, E])
        sw = sb("sw", [P, KT, E])
        wvt = sb("wvt", [P, KT, D])
        awt = sb("awt", [P, 2, KT])
        bvt = sb("bvt", [P, KT])
        bvb = sb("bvb", [P, KT, P])
        abt = sb("abt", [P, 1])
        cvec = sb("cvec", [P, NV])
        csum = sb("csum", [P, 2])
        cjs = sb("cjs", [P, 2])
        w12r = sb("w12r", [P, KT, 2 * D])
        w12h = sb("w12h", [P, KT, 2 * D], F32R)
        w12l = sb("w12l", [P, KT, 2 * D], F32R)
        w0r = sb("w0r", [P, KT, W0C])
        w0h = sb("w0h", [P, KT, W0C], F32R)
        w0l = sb("w0l", [P, KT, W0C], F32R)
        bkr = sb("bkr", [2, 3, D])
        bks = sb("bks", [2, 2, D])
        bkh = sb("bkh", [2, D], F32R)
        bkl = sb("bkl", [2, D], F32R)
        ebr = sb("ebr", [E, D])
        ebh = sb("ebh", [E, D], F32R)
        ebl = sb("ebl", [E, D], F32R)
        ebp = sb("ebp", [2, E * D], F32R)
        fill = sb("fill", [P, ROW])
        ewr = sb("ewr", [P, EWR, KT, D])
        ewh = sb("ewh", [P, E, KT, D], F32R)
        ewl = sb("ewl", [P, E, KT, D], F32R)

        xin = sb("xin", [P, BODY, D])
        ain = sb("ain", [P, BODY, N])
        rows = sb("rows", [P, BODY, ROW])
        od = sb("od", [P, 2 * G, D])
        st1 = sb("st1", [P, 2, 6])
        mv1 = sb("mv1", [P, 2 * G, 2])
        ve1 = sb("ve1", [P, 2, G])
        nm1 = sb("nm1", [P, 2, G])
        r1 = sb("r1", [P, 2, G])
        mhalf = sb("mhalf", [P, G])
        x0 = sb("x0", [P, 2, D])
        xth = sb("xth", [P, 2, D], F32R)
        xtl = sb("xtl", [P, 2, D], F32R)
        svs = sb("svs", [P, 2, NV])
        e1 = sb("e1", [P, 2, N])
        e2 = sb("e2", [P, 2, N])
        em = sb("em", [P, 2, N])
        al = sb("al", [P, 2, N])
        rs = sb("rs", [P, 2])
        ri = sb("ri", [P, 2])
        tm = sb("tm", [P, 2, N])
        tth = sb("tth", [P, 2, N], F32R)
        ttl = sb("ttl", [P, 2, N], F32R)
        z2h = sb("z2h", [P, 2, D], F32R)
        z2l = sb("z2l", [P, 2, D], F32R)
        z1h = sb("z1h", [P, 2, D], F32R)
        z1l = sb("z1l", [P, 2, D], F32R)
        st2 = sb("st2", [P, 2, 6])
        mv2 = sb("mv2", [P, 2, 2])
        ve2 = sb("ve2", [P, 2])
        nm2 = sb("nm2", [P, BODY])
        xf = sb("xf", [P, 2, D])
        xft = sb("xft", [P, D])
        lg = sb("lg", [P, G, E])
        mx = sb("mx", [P, G])
        df = sb("df", [P, G, E])
        wr = sb("wr", [P, G, E])
        mr = sb("mr", [P, 2, G])
        ex = sb("ex", [P, G, E])
        sx = sb("sx", [P, G])
        oh = sb("oh", [P, 2, G, E], BF16)
        pos = sb("pos", [P, 2, (G + 1) * E])
        sel = sb("sel", [P, G, E])
        slot = sb("slot", [P, G])
        far = sb("far", [P, G])
        idx = sb("idx", [P, 2 * G], U32)
        pr = sb("pr", [P, G])
        oa = sb("oa", [P, 2, G])
        oc = sb("oc", [P, 2, G])

        rin = rows[:, 0:TPE, :]
        yo = od[:, 0:HALF, :]
        tok = sb("tok", [P, HALF], U32)

        d_w = sem("d_w")
        d_small = sem("d_small")
        d_ew = [sem(f"d_ew{q}") for q in range(EWR)]
        d_x = [sem(f"d_x{q}") for q in range(NB)]
        d_fill = [sem(f"d_fill{q}") for q in range(3)]
        d_scat = [sem(f"d_scat{q}") for q in range(NB)]
        d_out = [sem(f"d_out{q}") for q in range(2)]
        s_fill = sem("s_fill")
        s_passed = sem("s_passed")
        s_pc = sem("s_pc")
        s_vc = sem("s_vc")
        s_pe0 = sem("s_pe0")
        s_st1 = sem("s_st1")
        s_mv1 = sem("s_mv1")
        s_ve1 = sem("s_ve1")
        s_r1 = sem("s_r1")
        s_x0 = sem("s_x0")
        s_x0t = sem("s_x0t")
        s_x0h = sem("s_x0h")
        s_x0l = sem("s_x0l")
        s_z0 = sem("s_z0")
        s_sv = sem("s_sv")
        s_z12 = sem("s_z12")
        s_z2h = sem("s_z2h")
        s_z2l = sem("s_z2l")
        s_st = sem("s_st")
        s_e = sem("s_e")
        s_em = sem("s_em")
        s_al = sem("s_al")
        s_ri = sem("s_ri")
        s_tm = sem("s_tm")
        s_tt = sem("s_tt")
        s_tth = sem("s_tth")
        s_ttl = sem("s_ttl")
        s_tz2 = sem("s_tz2")
        s_z1h = sem("s_z1h")
        s_z1l = sem("s_z1l")
        s_tz1 = sem("s_tz1")
        s_x1 = sem("s_x1")
        s_st2 = sem("s_st2")
        s_mv2 = sem("s_mv2")
        s_ve2 = sem("s_ve2")
        s_r2 = sem("s_r2")
        s_xf = sem("s_xf")
        s_xft = sem("s_xft")
        s_xfe = sem("s_xfe")
        s_log = sem("s_log")
        s_lgr = sem("s_lgr")
        s_ro = sem("s_ro")
        s_df = sem("s_df")
        s_ex = sem("s_ex")
        s_oh = sem("s_oh")
        s_pre = sem("s_pre")
        s_pos = sem("s_pos")
        s_slot = sem("s_slot")
        s_tok = sem("s_tok")
        s_odw = sem("s_odw")
        s_ewh = sem("s_ewh")
        s_ewl = sem("s_ewl")
        d_row = [sem(f"d_row{h}") for h in range(2)]
        b_xf = sem("b_xf")
        b_xt = sem("b_xt")
        b_hi = sem("b_hi")
        b_lo = sem("b_lo")
        b_y = sem("b_y")
        b_fin = sem("b_fin")
        b_sc = [sem(f"b_sc{r}") for r in range(HALF)]

        RO1, RO2 = 4, 8
        block = ctx.enter_context(nc.Block())

        def phase_a(eng, slot_fn, first, last):
            def run(it, lo, hi):
                for k in range(lo, hi):
                    slot_fn(it, k)
            run(0, first, BODY)
            with eng.Fori(1, PASSES - 1) as it:
                run(it, 0, BODY)
            run(PASSES - 1, 0, BODY + last)

        def valid(it, rel):
            return not isinstance(it, int) or 0 <= it * BODY + rel < B

        def ge(eng, s, value):
            if not isinstance(value, int) or value > 0:
                eng.wait_ge(s, value)

        def alone(eng):
            eng.sem_inc(s_passed, 1)

        def bat(it, rel):
            return it * NB + rel // G

        def phase_b(eng, tile):
            for i in range(TPE):
                tile(0, i, False)
            with eng.Fori(1, E - 1) as e:
                for i in range(TPE):
                    tile(e, i, False)
            for i in range(TPE):
                tile(E - 1, i, True)

        def experts_at(k):
            if E // 2 <= k < BODY:
                return [k - E // 2]
            if BODY < k <= BODY + E // 4:
                return [E // 2 + 2 * (k - BODY - 1), E // 2 + 2 * (k - BODY - 1) + 1]
            return []

        @block.sync
        def _(sp):
            xd = x.rearrange("(c g) n d -> c n g d", g=G)
            ad = adj.rearrange("(c g) n m -> c n g m", g=G)
            outd = out.rearrange("(c g) n d -> c n g d", g=G)

            def load(c, q):
                sp.dma_start(xin[:, q * G:(q + 1) * G, :], xd[c]).then_inc(d_x[q], 16)
                sp.dma_start(ain[:, q * G:(q + 1) * G, :], ad[c]).then_inc(d_x[q], 16)

            load(0, 0)
            for kt in range(KT):
                ks = slice(kt * P, (kt + 1) * P)
                sp.dma_start(w12r[:, kt, 0:D], Wk[2, ks, :]).then_inc(d_w, 16)
                sp.dma_start(w12r[:, kt, D:2 * D], Wk[1, ks, :]).then_inc(d_w, 16)
                sp.dma_start(w0r[:, kt, 0:D], Wk[0, ks, :]).then_inc(d_w, 16)
            sp.dma_start(wvt[:], WvT.rearrange("(t p) d -> p t d", p=P)).then_inc(d_w, 16)
            sp.dma_start(awt[:], aw.rearrange("p (h t) -> p h t", h=2)).then_inc(d_w, 16)
            sp.dma_start(bvt[:], bv).then_inc(d_w, 16)
            sp.dma_start(abt[:], ab.rearrange("(a o) -> a o", a=1).to_broadcast([P, 1])).then_inc(d_w, 16)
            sp.dma_start(swb[:], sb_.rearrange("(a o) -> a o", a=1).to_broadcast([P, E])).then_inc(d_w, 16)
            sp.dma_start(sw[:], swT.rearrange("(t p) e -> p t e", p=P)).then_inc(d_w, 16)
            for r in range(2):
                sp.dma_start(bkr[r:r + 1, :, :], bk.rearrange("(a k) d -> a k d", a=1)).then_inc(d_w, 16)
            sp.dma_start(ebr[:], eb).then_inc(d_w, 16)
            for q in range(1, NB):
                load(q, q)
            sp.wait_ge(s_vc, 8)
            sp.dma_start(bkh[1:2, :].bitcast(F32), bkl[0:1, :].bitcast(F32)).then_inc(d_small, 16)
            for e in range(E):
                sp.dma_start(ebp[0:1, e * D:(e + 1) * D].bitcast(F32), ebh[e:e + 1, :].bitcast(F32)).then_inc(d_small, 16)
                sp.dma_start(ebp[1:2, e * D:(e + 1) * D].bitcast(F32), ebl[e:e + 1, :].bitcast(F32)).then_inc(d_small, 16)

            def store(it, c, par):
                ge(sp, s_odw, it * BODY + (c + 1) * G)
                sp.dma_start(outd[it * NB + c], od[:, par * G:(par + 1) * G, :]).then_inc(d_out[par], 16)

            def one_pass(it, loads):
                for q in range(NB):
                    if valid(it, (q - 2) * G):
                        store(it, q - 2, q % 2)
                    if loads:
                        ge(sp, s_x1, it * BODY + (q + 1) * G)
                        load(it * NB + (q + NB), q)
                    elif q > 0:
                        for e in range(EWR * q, EWR * (q + 1)):
                            sp.wait_ge(s_ewl, e - EWR + 1)
                            load_expert(e)

            def load_expert(e):
                sp.dma_start(ewr[:, e % EWR], ewT[e].rearrange("(t p) f -> p t f", p=P)).then_inc(d_ew[e % EWR], 16)

            one_pass(0, True)
            with sp.Fori(1, PASSES - 1) as it:
                one_pass(it, True)
            for e in range(EWR):
                load_expert(e)
            one_pass(PASSES - 1, False)
            store(PASSES - 1, NB - 2, 0)
            store(PASSES - 1, NB - 1, 1)

            for q in range(NB):
                sp.wait_ge(d_scat[q], 16 * G * PASSES)
            rb = rowbuf.rearrange("(h p i e) r -> e h p i r", h=2, p=P, i=HALF)

            def load_rows(e, h):
                sp.dma_start(rin[:, h * HALF:(h + 1) * HALF, :], rb[e, h]).then_inc(d_row[h], 16)

            load_rows(0, 0)
            load_rows(0, 1)
            with sp.Fori(1, E) as e:
                for h in range(2):
                    sp.wait_ge(b_fin, e * TPE + (HALF * (h + 1) - TPE))
                    load_rows(e, h)
            for par in range(2):
                sp.wait_ge(d_out[par], 16 * (B // G // 2))
            for r in range(HALF):
                sp.wait_ge(b_sc[r], 16 * E * 2)

        @block.gpsimd
        def _(pool):
            pool.memset(fill[:], 0.0).then_inc(s_pc, 1)
            pool.wait_ge(s_pc, 1)
            pool.memset(fill[:, TOKEN:ROW], NOWHERE).then_inc(s_fill, 1)
            pool.memset(onesf[:], 1.0).then_inc(s_pc, 1)
            pool.memset(steps_bf[:], float(E)).then_inc(s_pc, 1)
            pool.memset(mhalf[:], -0.5).then_inc(s_pc, 1)
            pool.memset(cvec[:], 0.0).then_inc(s_pc, 1)
            pool.memset(w0r[:, :, D:W0C], 0.0).then_inc(s_pc, 1)
            pool.memset(ones2[:].bitcast(F32), 1.0).then_inc(s_pc, 1)
            pool.wait_ge(s_pc, 3)
            pool.affine_select(ident[:], onesf[:], pattern=[[1, P]], compare_op=ALU.is_equal, fill=0.0,
                               base=0, channel_multiplier=-1).then_inc(s_pc, 1)
            pool.affine_select(before_bf[:], steps_bf[:], pattern=[[1, P]], compare_op=ALU.is_gt, fill=0.0,
                               base=0, channel_multiplier=-1).then_inc(s_pc, 1)
            pool.iota(rev[:], pattern=[[0, G], [-1, E]], base=E, channel_multiplier=0,
                      allow_small_or_imprecise_dtypes=True).then_inc(s_pc, 1)
            pool.iota(pos[:, 1, G * E:(G + 1) * E], pattern=[[1, E]], base=0, channel_multiplier=0,
                      allow_small_or_imprecise_dtypes=True).then_inc(s_pc, 1)
            pool.iota(rows[:, 0:G, TOKEN], pattern=[[P, G]], base=0, channel_multiplier=1,
                      allow_small_or_imprecise_dtypes=True).then_inc(s_tok, 1)

            def slot_fn(it, k):
                g = k + LEAD_X0
                if valid(it, g):
                    q = g // G % 2
                    if g % G == 0:
                        pool.wait_ge(s_ve1, bat(it, g) + 1)
                        pool.tensor_tensor(r1[:, q, :], ve1[:, q, :], mhalf[:], ALU.pow).then_inc(s_r1, 1)
                        pool.wait_ge(s_r1, bat(it, g) + 1)
                    ge(pool, s_x0t, it * BODY + g - 1)
                    alone(pool)
                    pool.tensor_scalar(x0[:, g % 2, :], xin[:, g % BODY, :], nm1[:, q, g % G:g % G + 1],
                                       r1[:, q, g % G:g % G + 1], ALU.add, ALU.mult).then_inc(s_x0, 1)
                g = k - LAG_X1
                if valid(it, g):
                    r = g % BODY
                    pool.wait_ge(s_ve2, it * BODY + g + 1)
                    pool.tensor_tensor(rows[:, r, RSTD:RSTD + 1], ve2[:, g % 2:g % 2 + 1], mhalf[:, 0:1],
                                       ALU.pow).then_inc(s_r2, 1)
                    pool.wait_ge(s_r2, it * BODY + g + 1)
                    ge(pool, s_xft, it * BODY + g - 1)
                    alone(pool)
                    pool.tensor_scalar(xf[:, g % 2, :], rows[:, r, 0:D], nm2[:, r:r + 1],
                                       rows[:, r, RSTD:RSTD + 1], ALU.add, ALU.mult).then_inc(s_xf, 1)
                g = k - LAG_OUT
                if valid(it, g):
                    r = g % BODY
                    b2 = g // G % 2
                    i = b2 * G + g % G
                    if g % G == 0:
                        pool.wait_ge(s_slot, bat(it, g) + 1)
                        if not (isinstance(it, int) and it == 0 and g == 0):
                            pool.wait_ge(s_tok, bat(it, g))
                            alone(pool)
                            rp = (r - G) % BODY
                            pool.tensor_scalar(rows[:, r:r + G, TOKEN], rows[:, rp:rp + G, TOKEN],
                                               float(G * P), None, ALU.add).then_inc(s_tok, 1)
                        pool.wait_ge(s_tok, bat(it, g) + 1)
                        if isinstance(it, int) and it == 0 and g < 2 * G:
                            pool.wait_ge(d_fill[g // G], 16 * G)
                        ge(pool, d_out[b2], 16 * 2 * it + 16 * ((g // G - b2) // 2))
                        alone(pool)
                    limit = E * REG if not isinstance(it, int) or it > 0 else min(E * REG, E * P * G * (g // G + 1))
                    pool.indirect_dma_start(
                        out=rowbuf[0:limit], out_offset=bass.IndirectOffsetOnAxis(ap=idx[:, i:i + 1], axis=0),
                        in_=rows[:, r, :], in_offset=None, bounds_check=limit - 1, oob_is_err=False,
                    ).then_inc(d_scat[r // G], 16)
                    pool.tensor_scalar(od[:, i, :], rows[:, r, 0:D], oa[:, b2, g % G:g % G + 1],
                                       oc[:, b2, g % G:g % G + 1], ALU.mult, ALU.add).then_inc(s_odw, 1)

                if isinstance(it, int) and it == 0 and k == BODY - 1:
                    pool.wait_ge(d_fill[2], 16 * (TPE - 2 * G))

            phase_a(pool, slot_fn, -LEAD_X0, LAG_OUT)

            for par in range(2):
                pool.wait_ge(d_out[par], 16 * (B // G // 2))

            def send(e, i):
                pool.wait_ge(b_fin, e * TPE + i + 1)
                alone(pool)
                pool.indirect_dma_start(
                    out=out.rearrange("g n d -> (g n) d"),
                    out_offset=bass.IndirectOffsetOnAxis(ap=tok[:, i % HALF:i % HALF + 1], axis=0),
                    in_=yo[:, i % HALF, :], in_offset=None, bounds_check=TOK - 1, oob_is_err=False,
                ).then_inc(b_sc[i % HALF], 16)

            with pool.Fori(0, E) as e:
                for i in range(TPE):
                    send(e, i)

        @block.scalar
        def _(act):
            act.wait_ge(s_fill, 1)
            rbf = rowbuf.rearrange("(c p e) r -> c p e r", e=E, c=TPE)
            for c in range(TPE):
                act.dma_start(rbf[c], fill[:].rearrange("p (o r) -> p o r", o=1).to_broadcast([P, E, ROW])
                              ).then_inc(d_fill[min(c // G, 2)], 16)

            def slot_fn(it, k):
                g = k + LEAD_XT
                gx = k - LAG_XFT
                if valid(it, g):
                    act.wait_ge(s_x0t, it * BODY + g + 1)
                    act.copy(xth[:, g % 2, :], ps_xt[:, 0:D]).then_inc(s_x0h, 1)
                if valid(it, gx):
                    act.wait_ge(s_xft, it * BODY + gx + 1)
                    act.copy(xft[:], ps_xt[:, D:2 * D]).then_inc(s_xfe, 1)
                g = k - 1
                if valid(it, g):
                    act.wait_ge(s_tt, it * BODY + g + 1)
                    act.copy(tth[:, g % 2, :], ps_t[:, P:2 * P]).then_inc(s_tth, 1)
                    act.wait_ge(s_tz2, it * BODY + g + 1)
                    act.copy(z1h[:, g % 2, :], ps_z12[g % 2][:, D:2 * D]).then_inc(s_z1h, 1)
                g = k
                if valid(it, g):
                    act.wait_ge(s_st, it * BODY + g + 1)
                    ge(act, s_em, it * BODY + g - 1)
                    act.activation(e1[:, g % 2, :], ps_t[:, 0:P], ACT.Exp, bias=svs[:, g % 2, 1:2])
                    act.activation(e2[:, g % 2, :], ps_t[:, 0:P], ACT.Exp, bias=svs[:, g % 2, 2:3],
                                   scale=SLOPE).then_inc(s_e, 1)
                    act.wait_ge(s_z12, it * BODY + g + 1)
                    act.copy(z2h[:, g % 2, :], ps_z12[g % 2][:, 0:D]).then_inc(s_z2h, 1)
                g = k - LAG_ROUTE
                if g % G == 0 and valid(it, g):
                    act.wait_ge(s_df, bat(it, g) + 1)
                    act.activation(ex[:], df[:], ACT.Exp).then_inc(s_ex, 1)
                if isinstance(it, int) and it == PASSES - 1:
                    for e in experts_at(k):
                        act.wait_ge(d_ew[e % EWR], 16 * (1 + e // EWR))
                        act.copy(ewh[:, e], ewr[:, e % EWR]).then_inc(s_ewh, 1)

            phase_a(act, slot_fn, -LEAD_XT, LAG_OUT)

            def norm(e, i):
                act.wait_ge(d_row[i // HALF], e * 16 + 16) if i % HALF == 0 else None
                ge(act, b_xt, e * TPE + i - 1)
                act.activation(x0[:, i % 2, :], rin[:, i, 0:D], ACT.Identity, bias=rin[:, i, NMR:NMR + 1],
                               scale=rin[:, i, RSTD:RSTD + 1]).then_inc(b_xf, 1)

            def high(e, i):
                act.wait_ge(b_xt, e * TPE + i + 1)
                act.copy(xth[:, i % 2, :], ps_z12[i % 2][:, 0:D]).then_inc(b_hi, 1)

            norm(0, 0)
            norm(0, 1)

            def tile(e, i, last):
                if i + 2 < TPE:
                    norm(e, i + 2)
                elif not last:
                    norm(e + 1, i + 2 - TPE)
                high(e, i)

            phase_b(act, tile)

        @block.vector
        def _(dve):
            vc = [0]

            def link(ins):
                vc[0] += 1
                ins.then_inc(s_vc, 1)
                dve.wait_ge(s_vc, vc[0])

            dve.wait_ge(d_w, 16 * (3 * KT + 6 + 3))
            link(dve.tensor_tensor(bks[:, 0, :], bkr[:, 0, :], bkr[:, 1, :], ALU.add))
            link(dve.tensor_tensor(bks[:, 1, :], bks[:, 0, :], bkr[:, 2, :], ALU.add))
            link(dve.tensor_copy(bkh[:], bks[:, 1, :]))
            link(dve.tensor_tensor(bkl[:], bks[:, 1, :], bkh[:].bitcast(F32), ALU.subtract))
            link(dve.tensor_copy(ebh[:], ebr[:]))
            link(dve.tensor_tensor(ebl[:], ebr[:], ebh[:].bitcast(F32), ALU.subtract))
            dve.wait_ge(s_pc, 11)
            link(dve.tensor_scalar(bvb[:, 0, :], onesf[:], bvt[:, 0:1], None, ALU.mult))
            link(dve.tensor_scalar(bvb[:, 1, :], onesf[:], bvt[:, 1:2], None, ALU.mult))
            dve.wait_ge(s_pe0, 1)
            for kt in range(KT):
                link(dve.tensor_copy(w0r[:, kt, D:D + 2], ps_set[:, 2 * kt:2 * kt + 2]))
                link(dve.tensor_scalar(w0r[:, kt, D + 2:D + 3], w0r[:, kt, D + 1:D + 2], SLOPE, None, ALU.mult))
            link(dve.tensor_copy(cjs[:], ps_set[:, 2 * KT:2 * KT + 2]))
            link(dve.tensor_tensor(csum[:, 0:1], cjs[:, 0:1], cjs[:, 1:2], ALU.add))
            link(dve.tensor_tensor(cvec[:, 1:2], csum[:, 0:1], abt[:], ALU.add))
            link(dve.tensor_scalar(cvec[:, 2:3], cvec[:, 1:2], SLOPE, None, ALU.mult))
            link(dve.tensor_copy(w12h[:], w12r[:]))
            link(dve.tensor_tensor(w12l[:], w12r[:], w12h[:].bitcast(F32), ALU.subtract))
            link(dve.tensor_copy(w0h[:], w0r[:]))
            link(dve.tensor_tensor(w0l[:], w0r[:], w0h[:].bitcast(F32), ALU.subtract))

            ro = [0]

            def slot_fn(it, k):
                def n(rel):
                    return it * BODY + rel + 1

                g = k - LAG_X1
                if valid(it, g):
                    r = g % BODY
                    dve.wait_ge(s_tz1, n(g))
                    if g % G == 0:
                        ge(dve, d_scat[r // G], it * 16 * G + 16 * G * (g // BODY))
                    dve.scalar_tensor_tensor(rows[:, r, 0:D], ps_z0[g % 2][:, 0:D], 0.0, xin[:, r, :],
                                             ALU.max, ALU.add).then_inc(s_x1, 1)
                g = k + LEAD_STATS - 1
                if valid(it, g):
                    dve.wait_ge(s_st1, n(g))
                    alone(dve)
                    dve.bn_aggr(mv1[:, g % (2 * G), :], st1[:, g % 2, :]).then_inc(s_mv1, 1)
                g = k - LAG_X1
                if valid(it, g):
                    dve.wait_ge(s_x1, n(g))
                    dve.bn_stats(st2[:, g % 2, :], rows[:, g % BODY, 0:D]).then_inc(s_st2, 1)
                g = k + LEAD_XT
                if valid(it, g):
                    dve.wait_ge(s_x0h, n(g))
                    if valid(it, k - LAG_XFT):
                        dve.wait_ge(s_xfe, n(k - LAG_XFT))
                    dve.tensor_tensor(xtl[:, g % 2, :], ps_xt[:, 0:D], xth[:, g % 2, :].bitcast(F32),
                                      ALU.subtract).then_inc(s_x0l, 1)
                g = k - LAG_X1
                if valid(it, g):
                    dve.wait_ge(s_st2, n(g))
                    alone(dve)
                    dve.bn_aggr(mv2[:, g % 2, :], st2[:, g % 2, :]).then_inc(s_mv2, 1)
                g = k - 1
                if valid(it, g):
                    dve.wait_ge(s_tth, n(g))
                    dve.tensor_tensor(ttl[:, g % 2, :], ps_t[:, P:2 * P], tth[:, g % 2, :].bitcast(F32),
                                      ALU.subtract).then_inc(s_ttl, 1)
                g = k - LAG_X1
                if valid(it, g):
                    dve.wait_ge(s_mv2, n(g))
                    dve.tensor_scalar(nm2[:, g % BODY:g % BODY + 1], mv2[:, g % 2, 0:1], -1.0, None, ALU.mult)
                    dve.tensor_scalar(ve2[:, g % 2:g % 2 + 1], mv2[:, g % 2, 1:2], EPS, None,
                                      ALU.add).then_inc(s_ve2, 1)
                g = k + LEAD_STATS - G
                if g % G == 0 and valid(it, g):
                    q = g // G % 2
                    dve.wait_ge(s_mv1, n(g + G - 1))
                    dve.tensor_scalar(nm1[:, q, :], mv1[:, q * G:(q + 1) * G, 0], -1.0, None, ALU.mult)
                    dve.tensor_scalar(ve1[:, q, :], mv1[:, q * G:(q + 1) * G, 1], EPS, None,
                                      ALU.add).then_inc(s_ve1, 1)
                g = k
                if valid(it, g):
                    dve.wait_ge(s_z0, n(g))
                    dve.tensor_tensor(svs[:, g % 2, :], ps_z0[g % 2][:, D:W0C], cvec[:], ALU.add).then_inc(s_sv, 1)
                g = k - 1
                if valid(it, g):
                    dve.wait_ge(s_z1h, n(g))
                    dve.tensor_tensor(z1l[:, g % 2, :], ps_z12[g % 2][:, D:2 * D], z1h[:, g % 2, :].bitcast(F32),
                                      ALU.subtract).then_inc(s_z1l, 1)
                g = k + LEAD_STATS
                if valid(it, g):
                    if g % G == 0:
                        dve.wait_ge(d_x[g % BODY // G], 32 * it + 32 * (g // BODY) + 32)
                    dve.bn_stats(st1[:, g % 2, :], xin[:, g % BODY, :]).then_inc(s_st1, 1)
                g = k
                c = g % 2
                if valid(it, g):
                    dve.wait_ge(s_e, n(g))
                    dve.tensor_tensor(em[:, c, :], e1[:, c, :], e2[:, c, :], ALU.max).then_inc(s_em, 1)
                gr = k - LAG_ROUTE - 1
                if gr % G == 0 and valid(it, gr):
                    b2 = gr // G % 2
                    dve.wait_ge(s_pre, bat(it, gr) + 1)
                    if not isinstance(it, int) or gr + it * BODY > 0:
                        dve.wait_ge(s_pos, bat(it, gr))
                    dve.tensor_tensor(
                        pos[:, b2, :].rearrange("p (g e) -> p g e", e=E),
                        ps_t[:, 2 * P:2 * P + (G + 1) * E].rearrange("p (g e) -> p g e", e=E),
                        pos[:, 1 - b2, G * E:(G + 1) * E].rearrange("p (o e) -> p o e", o=1)
                        .to_broadcast([P, G + 1, E]), ALU.add).then_inc(s_pos, 1)
                if valid(it, g):
                    dve.wait_ge(s_em, n(g))
                    dve.tensor_tensor_reduce(al[:, c, :], ain[:, g % BODY, :], em[:, c, :], 1.0, ROW_EPS,
                                             ALU.mult, ALU.add, rs[:, c:c + 1]).then_inc(s_al, 1)
                    dve.wait_ge(s_al, n(g))
                    dve.reciprocal(ri[:, c:c + 1], rs[:, c:c + 1]).then_inc(s_ri, 1)
                    dve.wait_ge(s_ri, n(g))
                    dve.tensor_scalar(tm[:, c, :], al[:, c, :], ri[:, c:c + 1], None, ALU.mult).then_inc(s_tm, 1)
                    dve.wait_ge(s_z2h, n(g))
                    dve.tensor_tensor(z2l[:, c, :], ps_z12[c][:, 0:D], z2h[:, c, :].bitcast(F32),
                                      ALU.subtract).then_inc(s_z2l, 1)
                g = k - LAG_ROUTE
                if g % G == 0 and valid(it, g):
                    route(it, g)
                if gr % G == 0 and valid(it, gr):
                    place(it, gr)
                if isinstance(it, int) and it == PASSES - 1:
                    for e in experts_at(k):
                        dve.wait_ge(s_ewh, e + 1)
                        dve.tensor_tensor(ewl[:, e], ewr[:, e % EWR], ewh[:, e].bitcast(F32),
                                          ALU.subtract).then_inc(s_ewl, 1)

            def over_experts(v):
                return v.rearrange("p (g o) -> p g o", o=1).to_broadcast([P, G, E])

            NRO = 12

            def route(it, g):
                b = bat(it, g)
                b2 = g // G % 2
                dve.wait_ge(s_log, b + 1)
                lgp = ps_lg[:, 0:G * E].rearrange("p (g e) -> p g e", e=E)
                dve.tensor_tensor(lg[:], lgp, swb[:].rearrange("p (o e) -> p o e", o=1).to_broadcast([P, G, E]),
                                  ALU.add).then_inc(s_lgr, 1)
                dve.wait_ge(s_lgr, b + 1)
                dve.tensor_reduce(mx[:], lg[:], AX_X, ALU.max).then_inc(s_ro, 1)
                dve.wait_ge(s_ro, b * NRO + 1)
                dve.tensor_tensor(df[:], lg[:], over_experts(mx[:]), ALU.subtract).then_inc(s_df, 1)
                dve.wait_ge(s_df, b + 1)
                dve.scalar_tensor_tensor(wr[:], df[:], 0.0, rev[:], ALU.is_equal, ALU.mult).then_inc(s_ro, 1)
                dve.wait_ge(s_ro, b * NRO + 2)
                dve.tensor_reduce(mr[:, b2, :], wr[:], AX_X, ALU.max).then_inc(s_ro, 1)
                dve.wait_ge(s_ro, b * NRO + 3)
                dve.tensor_tensor(oh[:, b2], rev[:], over_experts(mr[:, b2, :]), ALU.is_equal).then_inc(s_oh, 1)

            def place(it, g):
                b = bat(it, g)
                b2 = g // G % 2
                r = g % BODY
                f = rows[:, r:r + G, :]
                dve.wait_ge(s_ex, b + 1)
                dve.tensor_reduce(sx[:], ex[:], AX_X, ALU.add).then_inc(s_ro, 1)
                dve.wait_ge(s_pos, b + 1)
                dve.wait_ge(s_oh, b + 1)
                dve.tensor_tensor(sel[:], oh[:, b2], pos[:, b2, 0:G * E].rearrange("p (g e) -> p g e", e=E),
                                  ALU.mult).then_inc(s_ro, 1)
                dve.wait_ge(s_ro, b * NRO + 4)
                dve.reciprocal(f[:, :, PROB], sx[:]).then_inc(s_ro, 1)
                dve.wait_ge(s_ro, b * NRO + 5)
                dve.tensor_reduce(slot[:], sel[:], AX_X, ALU.add).then_inc(s_ro, 1)
                dve.wait_ge(s_r2, it * BODY + g + G)
                dve.tensor_tensor(f[:, :, NMR], nm2[:, r:r + G], f[:, :, RSTD], ALU.mult).then_inc(s_ro, 1)
                dve.wait_ge(s_ro, b * NRO + 7)
                dve.tensor_scalar(far[:], slot[:], float(E * CAP), NOWHERE, ALU.is_ge, ALU.mult).then_inc(s_ro, 1)
                dve.tensor_tensor(pr[:], f[:, :, PROB], f[:, :, RSTD], ALU.mult).then_inc(s_ro, 1)
                dve.wait_ge(s_ro, b * NRO + 8)
                ge(dve, s_odw, it * BODY + g - G)
                dve.tensor_tensor(oc[:, b2, :], f[:, :, PROB], f[:, :, NMR], ALU.mult).then_inc(s_ro, 1)
                dve.wait_ge(s_ro, b * NRO + 10)
                dve.tensor_scalar(oa[:, b2, :], pr[:], 1.0, None, ALU.add).then_inc(s_ro, 1)
                dve.wait_ge(s_ro, b * NRO + 9)
                ge(dve, d_scat[(r // G - 2) % NB], it * 16 * G + 16 * G * ((g // G - 2) // NB + 1))
                dve.scalar_tensor_tensor(idx[:, b2 * G:(b2 + 1) * G], far[:], 1.0, slot[:], ALU.mult,
                                         ALU.add).then_inc(s_slot, 1)

            phase_a(dve, slot_fn, -LEAD_STATS, LAG_OUT)

            def low(e, i):
                dve.wait_ge(b_hi, e * TPE + i + 1)
                dve.tensor_tensor(xtl[:, i % 2, :], ps_z12[i % 2][:, 0:D], xth[:, i % 2, :].bitcast(F32),
                                  ALU.subtract).then_inc(b_lo, 1)

            def finish(e, i):
                h = i % HALF
                dve.wait_ge(b_y, e * TPE + i + 1)
                ge(dve, b_sc[h], e * 32 + 16 * (i // HALF))
                dve.tensor_copy(tok[:, h:h + 1], rin[:, i, TOKEN:ROW])
                dve.scalar_tensor_tensor(yo[:, h, :], ps_z0[i % 2][:, 0:D], rin[:, i, PROB:PROB + 1],
                                         rin[:, i, 0:D], ALU.mult, ALU.add).then_inc(b_fin, 1)

            for par in range(2):
                dve.wait_ge(d_out[par], 16 * (B // G // 2))
            low(0, 0)

            def tile(e, i, last):
                if i + 1 < TPE:
                    low(e, i + 1)
                elif not last:
                    low(e + 1, 0)
                finish(e, i)

            phase_b(dve, tile)

        @block.tensor
        def _(pe):
            pe.wait_ge(d_w, 16 * (3 * KT + 6 + 3))
            pe.wait_ge(s_vc, 8)
            for kt in range(KT):
                for t in range(KT):
                    pe.matmul(ps_set[:, 2 * kt:2 * kt + 2], wvt[:, t, kt * P:(kt + 1) * P], awt[:, :, t],
                              start=(t == 0), stop=(t == KT - 1))
            for t in range(KT):
                mm = pe.matmul(ps_set[:, 2 * KT:2 * KT + 2], bvb[:, t, :], awt[:, :, t],
                               start=(t == 0), stop=(t == KT - 1))
            mm.then_inc(s_pe0, 1)
            pe.wait_ge(d_small, 16 * (1 + 2 * E))
            pe.wait_ge(s_vc, 20)

            def products(psum_out, lhs_h, lhs_l, rhs_h, rhs_l, tiles, start):
                steps = [(l, r, t) for l, r in ((lhs_h, rhs_h), (lhs_h, rhs_l), (lhs_l, rhs_h)) for t in tiles]
                for n_, (l, r, t) in enumerate(steps):
                    yield lambda l=l, r=r, t=t, n_=n_: pe.matmul(
                        psum_out, l(t), r(t), start=start and n_ == 0, stop=n_ == len(steps) - 1,
                        skip_group_check=True)

            def slot_fn(it, k):
                def n(rel):
                    return it * BODY + rel + 1

                gx = k - LAG_XFT
                g = k + LEAD_XT
                if valid(it, k) and not (isinstance(it, int) and it == 0 and k == 0 and False):
                    ge(pe, s_x0l, n(k))
                if valid(it, gx - 1):
                    pe.wait_ge(s_xfe, n(gx - 1))
                if valid(it, gx):
                    pe.wait_ge(s_xf, n(gx))
                    for t in range(KT):
                        mm = pe.transpose(ps_xt[:, D + t * P:D + (t + 1) * P], xf[:, gx % 2, t * P:(t + 1) * P],
                                          ident[:])
                    mm.then_inc(s_xft, 1)
                if valid(it, g):
                    pe.wait_ge(s_x0, n(g))
                    for t in range(KT):
                        mm = pe.transpose(ps_xt[:, t * P:(t + 1) * P], x0[:, g % 2, t * P:(t + 1) * P], ident[:])
                    mm.then_inc(s_x0t, 1)
                c = k % 2
                z12 = []
                if valid(it, k):
                    if valid(it, k - 2):
                        pe.wait_ge(s_z1l, n(k - 2))
                    z12 = list(products(ps_z12[c][:], lambda t: xth[:, c, t * P:(t + 1) * P],
                                        lambda t: xtl[:, c, t * P:(t + 1) * P], lambda t: w12h[:, t, :],
                                        lambda t: w12l[:, t, :], range(KT), True))
                    for f in z12[:3]:
                        f()
                g = k - 1
                d = g % 2
                if valid(it, g):
                    pe.wait_ge(s_tm, n(g))
                    gr = k - LAG_ROUTE - 2
                    if gr % G == 0 and valid(it, gr):
                        pe.wait_ge(s_pos, bat(it, gr) + 1)
                    pe.transpose(ps_t[:, P:2 * P], tm[:, d, :], ident[:]).then_inc(s_tt, 1)
                if valid(it, k):
                    if valid(it, k - 2):
                        pe.wait_ge(s_x1, n(k - 2))
                    for f in products(ps_z0[c][:, 0:W0C], lambda t: xth[:, c, t * P:(t + 1) * P],
                                      lambda t: xtl[:, c, t * P:(t + 1) * P], lambda t: w0h[:, t, :],
                                      lambda t: w0l[:, t, :], range(KT), True):
                        mm = f()
                    mm.then_inc(s_z0, 1)
                if valid(it, g):
                    pe.wait_ge(s_ttl, n(g))
                    pe.wait_ge(s_z2l, n(g))
                    for f in products(ps_z12[d][:, D:2 * D], lambda t: tth[:, d, :], lambda t: ttl[:, d, :],
                                      lambda t: z2h[:, d, :], lambda t: z2l[:, d, :], [0], False):
                        mm = f()
                    mm.then_inc(s_tz2, 1)
                gr = k - LAG_ROUTE - 1
                if gr % G == 0 and valid(it, gr):
                    b2 = gr // G % 2
                    pe.wait_ge(s_oh, bat(it, gr) + 1)
                    if not valid(it, g):
                        pe.wait_ge(s_pos, bat(it, gr))
                    ohf = oh[:, b2].rearrange("p g e -> p (g e)")
                    o = 2 * P
                    for sh in range(1, G + 1):
                        pe.matmul(ps_t[:, o + sh * E:o + (G + 1) * E], steps_bf[:], ohf[:, 0:(G + 1 - sh) * E],
                                  start=(sh == 1), stop=False, skip_group_check=True)
                    pe.matmul(ps_t[:, o:o + G * E], before_bf[:], ohf, start=False, stop=True,
                              skip_group_check=True).then_inc(s_pre, 1)
                if valid(it, k):
                    pe.wait_ge(s_sv, n(k))
                    pe.transpose(ps_t[:, 0:P], svs[:, c, 0:1].to_broadcast([P, P]), ident[:]).then_inc(s_st, 1)
                    for f in z12[3:]:
                        mm = f()
                    mm.then_inc(s_z12, 1)
                if valid(it, gx):
                    j = gx % G
                    pe.wait_ge(s_xfe, n(gx))
                    if j == 0:
                        ge(pe, s_lgr, bat(it, gx))
                    for t in range(KT):
                        mm = pe.matmul(ps_lg[:, j * E:(j + 1) * E], xft[:, t * P:(t + 1) * P], sw[:, t, :],
                                       start=(t == 0), stop=(t == KT - 1), skip_group_check=True)
                    if j == G - 1:
                        mm.then_inc(s_log, 1)
                if valid(it, g):
                    pe.wait_ge(s_z1l, n(g))
                    for f in products(ps_z0[d][:, 0:D], lambda t: tth[:, d, :], lambda t: ttl[:, d, :],
                                      lambda t: z1h[:, d, :], lambda t: z1l[:, d, :], [0], False):
                        f()
                    pe.matmul(ps_z0[d][:, 0:D], ones2[:], bkh[:], start=False, stop=True,
                              skip_group_check=True).then_inc(s_tz1, 1)

            phase_a(pe, slot_fn, -LEAD_XT, LAG_OUT)

            def turn(e, i):
                pe.wait_ge(b_xf, e * TPE + i + 1)
                ge(pe, b_lo, e * TPE + i - 1)
                for t in range(KT):
                    mm = pe.transpose(ps_z12[i % 2][:, t * P:(t + 1) * P], x0[:, i % 2, t * P:(t + 1) * P], ident[:])
                mm.then_inc(b_xt, 1)

            def expert(e, i):
                pe.wait_ge(b_lo, e * TPE + i + 1)
                ge(pe, b_fin, e * TPE + i - 1)
                c = i % 2
                y = ps_z0[c][:, 0:D]
                for f in products(y, lambda t: xth[:, c, t * P:(t + 1) * P], lambda t: xtl[:, c, t * P:(t + 1) * P],
                                  lambda t: wof(ewh, e, t), lambda t: wof(ewl, e, t), range(KT), True):
                    f()
                eo = e * D
                pe.matmul(y, ones2[:], ebp[:, bass.ds(eo, D)], start=False, stop=True,
                          skip_group_check=True).then_inc(b_y, 1)

            def wof(w, e, t):
                return w[:].rearrange("p e t f -> p (e t f)")[:, bass.ds(e * (KT * D) + t * D, D)]

            turn(0, 0)

            def tile(e, i, last):
                if i + 1 < TPE:
                    turn(e, i + 1)
                elif not last:
                    turn(e + 1, 0)
                expert(e, i)

            pe.wait_ge(s_ewl, E)
            phase_b(pe, tile)


def kernel(x, adj, L0_gnn_Wv, L0_gnn_bv, L0_gnn_aw, L0_gnn_ab, L0_gnn_Wk, L0_gnn_bk, L0_ffn_switch_w,
           L0_ffn_switch_b, L0_ffn_expert_w, L0_ffn_expert_b):
    import numpy as np
    import concourse.bacc as bacc
    from concourse import mybir
    from concourse.bass_utils import run_bass_kernel_spmd

    ins = {
        "x": x, "adj": adj, "WvT": np.transpose(L0_gnn_Wv), "bv": np.transpose(np.reshape(L0_gnn_bv, (-1, P))),
        "aw": np.transpose(np.reshape(L0_gnn_aw, (-1, P))), "ab": L0_gnn_ab,
        "Wk": L0_gnn_Wk, "bk": L0_gnn_bk, "swT": np.transpose(L0_ffn_switch_w), "sb": L0_ffn_switch_b,
        "ewT": np.transpose(L0_ffn_expert_w, (0, 2, 1)), "eb": L0_ffn_expert_b,
    }
    nc = bacc.Bacc("TRN2", target_bir_lowering=False, num_devices=1)
    arrays, args = {}, []
    for name, a in ins.items():
        a = np.ascontiguousarray(a)
        arrays[f"in_{name}"] = a
        args.append(nc.dram_tensor(f"in_{name}", a.shape, mybir.dt.from_np(a.dtype), kind="ExternalInput").ap())
    out = nc.dram_tensor("out_0", list(x.shape), mybir.dt.float32, kind="ExternalOutput").ap()
    graph_then_experts(nc, *args, out)
    r = run_bass_kernel_spmd(nc, [arrays], core_ids=[0])
    return r.results[0]["out_0"]
```

```python
from contextlib import ExitStack

import concourse.bass as bass
from concourse import mybir

P = 128
ALU = mybir.AluOpType
ACT = mybir.ActivationFunctionType
F32 = mybir.dt.float32
F32R = mybir.dt.float32r
BF16 = mybir.dt.bfloat16
U32 = mybir.dt.uint32
AX_X = mybir.AxisListType.X

EPS = 1e-5
ROW_EPS = 1e-12
SLOPE = 0.2
CAPACITY_FACTOR = 1.2
BODY = 16
G = 4
NOWHERE = 1.0e6

LAG_X1 = 2
LAG_XFT = 3
LAG_ROUTE = 7
LAG_OUT = 9
LEAD_STATS = 7
LEAD_X0 = 2
LEAD_XT = 1


def graph_then_experts(nc, x, adj, WvT, bv, aw, ab, Wk, bk, swT, sb_, ewT, eb, out):
    B, N, D = x.shape
    KT = D // P
    E = swT.shape[1]
    TOK = B * N
    CAP = int(CAPACITY_FACTOR * TOK / E)
    TPE = -(-CAP // P)
    REG = TPE * P
    HALF = TPE // 2
    ROW = D + 4
    NMR, RSTD, PROB, TOKEN = D, D + 1, D + 2, D + 3
    NV = 4
    W0C = D + NV
    PASSES = B // BODY
    RB, RY = 4, 5
    EWR = 4
    NB = BODY // G
    assert N == P and TPE % 2 == 0 and Wk.shape[0] == 3 and B % BODY == 0

    rowbuf = nc.dram_tensor("rowbuf", [E * REG, ROW], F32, kind="Internal").ap()

    with ExitStack() as ctx:
        def sb(name, shape, dt=F32):
            return ctx.enter_context(nc.sbuf_tensor(name, shape, dt))

        def psum(name):
            return ctx.enter_context(nc.psum_tensor(name, [P, 512], F32))

        def sem(name):
            return ctx.enter_context(nc.semaphore(name))

        ps_z0 = [psum("ps_z0a"), psum("ps_z0b")]
        ps_z12 = [psum("ps_z12a"), psum("ps_z12b")]
        ps_xt = psum("ps_xt")
        ps_t = psum("ps_t")
        ps_lg = [psum("ps_lga"), psum("ps_lgb")]
        ps_set = ps_lg[1]
        ps_bx = [*ps_z12, ps_xt, ps_t]
        ps_by = [*ps_z0, *ps_lg]

        ident = sb("ident", [P, P])
        onesf = sb("onesf", [P, P])
        steps_bf = sb("steps_bf", [P, P], BF16)
        before_bf = sb("before_bf", [P, P], BF16)
        ones2 = sb("ones2", [2, P], F32R)
        rev = sb("rev", [P, G, E])
        swb = sb("swb", [P, E])
        sw = sb("sw", [P, KT, E])
        wvt = sb("wvt", [P, KT, D])
        awt = sb("awt", [P, 2, KT])
        bvt = sb("bvt", [P, KT])
        bvb = sb("bvb", [P, KT, P])
        abt = sb("abt", [P, 1])
        cvec = sb("cvec", [P, NV])
        csum = sb("csum", [P, 2])
        cjs = sb("cjs", [P, 2])
        w12r = sb("w12r", [P, KT, 2 * D])
        w12h = sb("w12h", [P, KT, 2 * D], F32R)
        w12l = sb("w12l", [P, KT, 2 * D], F32R)
        w0r = sb("w0r", [P, KT, W0C])
        w0h = sb("w0h", [P, KT, W0C], F32R)
        w0l = sb("w0l", [P, KT, W0C], F32R)
        bkr = sb("bkr", [2, 3, D])
        bks = sb("bks", [2, 2, D])
        bkh = sb("bkh", [2, D], F32R)
        bkl = sb("bkl", [2, D], F32R)
        ebr = sb("ebr", [E, D])
        ebh = sb("ebh", [E, D], F32R)
        ebl = sb("ebl", [E, D], F32R)
        ebp = sb("ebp", [2, E * D], F32R)
        fill = sb("fill", [P, ROW])
        ewr = sb("ewr", [P, EWR, KT, D])
        ewh = sb("ewh", [P, E, KT, D], F32R)
        ewl = sb("ewl", [P, E, KT, D], F32R)

        xin = sb("xin", [P, BODY, D])
        ain = sb("ain", [P, BODY, N])
        rows = sb("rows", [P, 2 * TPE, ROW])
        od = sb("od", [P, 2 * G, D])
        st1 = sb("st1", [P, 2, 6])
        mv1 = sb("mv1", [P, 2 * G, 2])
        ve1 = sb("ve1", [P, 2, G])
        nm1 = sb("nm1", [P, 2, G])
        r1 = sb("r1", [P, 2, G])
        mhalf = sb("mhalf", [P, G])
        x0 = sb("x0", [P, RB, D])
        xth = sb("xth", [P, RB, D], F32R)
        xtl = sb("xtl", [P, RB, D], F32R)
        svs = sb("svs", [P, 2, NV])
        e1 = sb("e1", [P, 2, N])
        e2 = sb("e2", [P, 2, N])
        em = sb("em", [P, 2, N])
        al = sb("al", [P, 2, N])
        rs = sb("rs", [P, 2])
        ri = sb("ri", [P, 2])
        tm = sb("tm", [P, 2, N])
        tt = sb("tt", [P, 2, N])
        z2 = sb("z2", [P, 2, D])
        z1 = sb("z1", [P, 2, D])
        st2 = sb("st2", [P, 2, 6])
        mv2 = sb("mv2", [P, 2, 2])
        ve2 = sb("ve2", [P, 2])
        nm2 = sb("nm2", [P, BODY])
        xf = sb("xf", [P, 2, D])
        xft = sb("xft", [P, D])
        lg = sb("lg", [P, G, E])
        mx = sb("mx", [P, G])
        df = sb("df", [P, G, E])
        wr = sb("wr", [P, G, E])
        mr = sb("mr", [P, G])
        ex = sb("ex", [P, G, E])
        sx = sb("sx", [P, G])
        oh = sb("oh", [P, 2, G, E], BF16)
        pos = sb("pos", [P, 2, (G + 1) * E])
        sel = sb("sel", [P, G, E])
        slot = sb("slot", [P, G])
        far = sb("far", [P, G])
        idx = sb("idx", [P, 2 * G], U32)
        pr = sb("pr", [P, G])
        oa = sb("oa", [P, 2, G])
        oc = sb("oc", [P, 2, G])

        rin = rows
        yo = od[:, 0:RY, :]
        tok = sb("tok", [P, RY], U32)

        d_w = sem("d_w")
        d_small = sem("d_small")
        d_ew = [sem(f"d_ew{q}") for q in range(EWR)]
        d_x = [sem(f"d_x{q}") for q in range(NB)]
        d_fill = [sem(f"d_fill{q}") for q in range(3)]
        d_scat = [sem(f"d_scat{q}") for q in range(NB)]
        d_out = [sem(f"d_out{q}") for q in range(2)]
        s_fill = sem("s_fill")
        s_passed = sem("s_passed")
        s_pc = sem("s_pc")
        s_vc = sem("s_vc")
        s_pe0 = sem("s_pe0")
        s_st1 = sem("s_st1")
        s_mv1 = sem("s_mv1")
        s_ve1 = sem("s_ve1")
        s_r1 = sem("s_r1")
        s_x0 = sem("s_x0")
        s_x0t = sem("s_x0t")
        s_x0h = sem("s_x0h")
        s_x0l = sem("s_x0l")
        s_z0 = sem("s_z0")
        s_sv = sem("s_sv")
        s_z12 = sem("s_z12")
        s_z2 = sem("s_z2")
        s_st = sem("s_st")
        s_e = sem("s_e")
        s_em = sem("s_em")
        s_al = sem("s_al")
        s_ri = sem("s_ri")
        s_tm = sem("s_tm")
        s_tt = sem("s_tt")
        s_tte = sem("s_tte")
        s_tz2 = sem("s_tz2")
        s_z1 = sem("s_z1")
        s_tz1 = sem("s_tz1")
        s_x1 = sem("s_x1")
        s_st2 = sem("s_st2")
        s_mv2 = sem("s_mv2")
        s_ve2 = sem("s_ve2")
        s_r2 = sem("s_r2")
        s_xf = sem("s_xf")
        s_xft = sem("s_xft")
        s_xfe = sem("s_xfe")
        s_log = sem("s_log")
        s_lgr = sem("s_lgr")
        s_ro = sem("s_ro")
        s_df = sem("s_df")
        s_ex = sem("s_ex")
        s_oh = sem("s_oh")
        s_pre = sem("s_pre")
        s_pos = sem("s_pos")
        s_slot = sem("s_slot")
        s_tok = sem("s_tok")
        s_odw = sem("s_odw")
        s_ewh = sem("s_ewh")
        s_ewl = sem("s_ewl")
        d_row = [sem(f"d_row{h}") for h in range(4)]
        b_xf = sem("b_xf")
        b_xt = sem("b_xt")
        b_hi = sem("b_hi")
        b_lo = sem("b_lo")
        b_y = sem("b_y")
        b_fin = sem("b_fin")
        b_sc = [sem(f"b_sc{r}") for r in range(RY)]

        RO1, RO2 = 4, 8
        block = ctx.enter_context(nc.Block())

        def phase_a(eng, slot_fn, first, last):
            def run(it, lo, hi):
                for k in range(lo, hi):
                    slot_fn(it, k)
            run(0, first, BODY)
            with eng.Fori(1, PASSES - 1) as it:
                run(it, 0, BODY)
            run(PASSES - 1, 0, BODY + last)

        def valid(it, rel):
            return not isinstance(it, int) or 0 <= it * BODY + rel < B

        def ge(eng, s, value):
            if not isinstance(value, int) or value > 0:
                eng.wait_ge(s, value)

        def alone(eng):
            eng.sem_inc(s_passed, 1)

        def bat(it, rel):
            return it * NB + rel // G

        TB = 2 * TPE
        LAST = E * TPE // TB - 1

        def phase_b(eng, tile):
            for i in range(TB):
                tile(0, i)
            with eng.Fori(1, LAST) as u:
                for i in range(TB):
                    tile(u, i)
            for i in range(TB):
                tile(LAST, i)

        def ahead(u, i):
            return not (isinstance(u, int) and u == LAST and i >= TB)

        def experts_at(k):
            if E // 2 <= k < BODY:
                return [k - E // 2]
            if BODY < k <= BODY + E // 4:
                return [E // 2 + 2 * (k - BODY - 1), E // 2 + 2 * (k - BODY - 1) + 1]
            return []

        @block.sync
        def _(sp):
            xd = x.rearrange("(c g) n d -> c n g d", g=G)
            ad = adj.rearrange("(c g) n m -> c n g m", g=G)
            outd = out.rearrange("(c g) n d -> c n g d", g=G)

            def load(c, q):
                sp.dma_start(xin[:, q * G:(q + 1) * G, :], xd[c]).then_inc(d_x[q], 16)
                sp.dma_start(ain[:, q * G:(q + 1) * G, :], ad[c]).then_inc(d_x[q], 16)

            load(0, 0)
            for kt in range(KT):
                ks = slice(kt * P, (kt + 1) * P)
                sp.dma_start(w12r[:, kt, 0:D], Wk[2, ks, :]).then_inc(d_w, 16)
                sp.dma_start(w12r[:, kt, D:2 * D], Wk[1, ks, :]).then_inc(d_w, 16)
                sp.dma_start(w0r[:, kt, 0:D], Wk[0, ks, :]).then_inc(d_w, 16)
            sp.dma_start(wvt[:], WvT.rearrange("(t p) d -> p t d", p=P)).then_inc(d_w, 16)
            sp.dma_start(awt[:], aw.rearrange("p (h t) -> p h t", h=2)).then_inc(d_w, 16)
            sp.dma_start(bvt[:], bv).then_inc(d_w, 16)
            sp.dma_start(abt[:], ab.rearrange("(a o) -> a o", a=1).to_broadcast([P, 1])).then_inc(d_w, 16)
            sp.dma_start(swb[:], sb_.rearrange("(a o) -> a o", a=1).to_broadcast([P, E])).then_inc(d_w, 16)
            sp.dma_start(sw[:], swT.rearrange("(t p) e -> p t e", p=P)).then_inc(d_w, 16)
            for r in range(2):
                sp.dma_start(bkr[r:r + 1, :, :], bk.rearrange("(a k) d -> a k d", a=1)).then_inc(d_w, 16)
            sp.dma_start(ebr[:], eb).then_inc(d_w, 16)
            for q in range(1, NB):
                load(q, q)
            sp.wait_ge(s_vc, 8)
            sp.dma_start(bkh[1:2, :].bitcast(F32), bkl[0:1, :].bitcast(F32)).then_inc(d_small, 16)
            for e in range(E):
                sp.dma_start(ebp[0:1, e * D:(e + 1) * D].bitcast(F32), ebh[e:e + 1, :].bitcast(F32)).then_inc(d_small, 16)
                sp.dma_start(ebp[1:2, e * D:(e + 1) * D].bitcast(F32), ebl[e:e + 1, :].bitcast(F32)).then_inc(d_small, 16)

            def store(it, c, par):
                ge(sp, s_odw, it * BODY + (c + 1) * G)
                sp.dma_start(outd[it * NB + c], od[:, par * G:(par + 1) * G, :]).then_inc(d_out[par], 16)

            def one_pass(it, loads):
                for q in range(NB):
                    if valid(it, (q - 2) * G):
                        store(it, q - 2, q % 2)
                    if loads:
                        ge(sp, s_x1, it * BODY + (q + 1) * G)
                        load(it * NB + (q + NB), q)
                    elif q > 0:
                        for e in range(EWR * q, EWR * (q + 1)):
                            sp.wait_ge(s_ewl, e - EWR + 1)
                            load_expert(e)

            def load_expert(e):
                sp.dma_start(ewr[:, e % EWR], ewT[e].rearrange("(t p) f -> p t f", p=P)).then_inc(d_ew[e % EWR], 16)

            one_pass(0, True)
            with sp.Fori(1, PASSES - 1) as it:
                one_pass(it, True)
            for e in range(EWR):
                load_expert(e)
            one_pass(PASSES - 1, False)
            store(PASSES - 1, NB - 2, 0)
            store(PASSES - 1, NB - 1, 1)

            for q in range(NB):
                sp.wait_ge(d_scat[q], 16 * G * PASSES)
            rb = rowbuf.rearrange("(h p i e) r -> e h p i r", h=2, p=P, i=HALF)

            def load_rows(u, h):
                sp.dma_start(rin[:, h * HALF:(h + 1) * HALF, :], rb[u * 2 + h // 2, h % 2]).then_inc(d_row[h], 16)

            for h in range(4):
                load_rows(0, h)
            with sp.Fori(1, LAST + 1) as u:
                for h in range(4):
                    sp.wait_ge(b_fin, u * TB + (HALF * (h + 1) - TB))
                    load_rows(u, h)
            for par in range(2):
                sp.wait_ge(d_out[par], 16 * (B // G // 2))
            for r in range(RY):
                sp.wait_ge(b_sc[r], 16 * E * TPE // RY)

        @block.gpsimd
        def _(pool):
            pool.memset(fill[:], 0.0).then_inc(s_pc, 1)
            pool.wait_ge(s_pc, 1)
            pool.memset(fill[:, TOKEN:ROW], NOWHERE).then_inc(s_fill, 1)
            pool.memset(onesf[:], 1.0).then_inc(s_pc, 1)
            pool.memset(steps_bf[:], float(E)).then_inc(s_pc, 1)
            pool.memset(mhalf[:], -0.5).then_inc(s_pc, 1)
            pool.memset(cvec[:], 0.0).then_inc(s_pc, 1)
            pool.memset(w0r[:, :, D:W0C], 0.0).then_inc(s_pc, 1)
            pool.memset(ones2[:].bitcast(F32), 1.0).then_inc(s_pc, 1)
            pool.wait_ge(s_pc, 3)
            pool.affine_select(ident[:], onesf[:], pattern=[[1, P]], compare_op=ALU.is_equal, fill=0.0,
                               base=0, channel_multiplier=-1).then_inc(s_pc, 1)
            pool.affine_select(before_bf[:], steps_bf[:], pattern=[[1, P]], compare_op=ALU.is_gt, fill=0.0,
                               base=0, channel_multiplier=-1).then_inc(s_pc, 1)
            pool.iota(rev[:], pattern=[[0, G], [-1, E]], base=E, channel_multiplier=0,
                      allow_small_or_imprecise_dtypes=True).then_inc(s_pc, 1)
            pool.iota(pos[:, 1, G * E:(G + 1) * E], pattern=[[1, E]], base=0, channel_multiplier=0,
                      allow_small_or_imprecise_dtypes=True).then_inc(s_pc, 1)
            pool.iota(rows[:, 0:G, TOKEN], pattern=[[P, G]], base=0, channel_multiplier=1,
                      allow_small_or_imprecise_dtypes=True).then_inc(s_tok, 1)

            def slot_fn(it, k):
                g = k + LEAD_X0
                if valid(it, g):
                    q = g // G % 2
                    if g % G == 0:
                        pool.wait_ge(s_ve1, bat(it, g) + 1)
                        pool.tensor_tensor(r1[:, q, :], ve1[:, q, :], mhalf[:], ALU.pow).then_inc(s_r1, 1)
                        pool.wait_ge(s_r1, bat(it, g) + 1)
                    ge(pool, s_x0t, it * BODY + g - 1)
                    alone(pool)
                    pool.tensor_scalar(x0[:, g % 2, :], xin[:, g % BODY, :], nm1[:, q, g % G:g % G + 1],
                                       r1[:, q, g % G:g % G + 1], ALU.add, ALU.mult).then_inc(s_x0, 1)
                g = k - LAG_X1
                if valid(it, g):
                    r = g % BODY
                    pool.wait_ge(s_ve2, it * BODY + g + 1)
                    pool.tensor_tensor(rows[:, r, RSTD:RSTD + 1], ve2[:, g % 2:g % 2 + 1], mhalf[:, 0:1],
                                       ALU.pow).then_inc(s_r2, 1)
                    pool.wait_ge(s_r2, it * BODY + g + 1)
                    ge(pool, s_xft, it * BODY + g - 1)
                    alone(pool)
                    pool.tensor_scalar(xf[:, g % 2, :], rows[:, r, 0:D], nm2[:, r:r + 1],
                                       rows[:, r, RSTD:RSTD + 1], ALU.add, ALU.mult).then_inc(s_xf, 1)
                g = k - LAG_OUT
                if valid(it, g):
                    r = g % BODY
                    b2 = g // G % 2
                    i = b2 * G + g % G
                    if g % G == 0:
                        pool.wait_ge(s_slot, bat(it, g) + 1)
                        if not (isinstance(it, int) and it == 0 and g == 0):
                            pool.wait_ge(s_tok, bat(it, g))
                            alone(pool)
                            rp = (r - G) % BODY
                            pool.tensor_scalar(rows[:, r:r + G, TOKEN], rows[:, rp:rp + G, TOKEN],
                                               float(G * P), None, ALU.add).then_inc(s_tok, 1)
                        pool.wait_ge(s_tok, bat(it, g) + 1)
                        if isinstance(it, int) and it == 0 and g < 2 * G:
                            pool.wait_ge(d_fill[g // G], 16 * G)
                        ge(pool, d_out[b2], 16 * 2 * it + 16 * ((g // G - b2) // 2))
                        alone(pool)
                    limit = E * REG if not isinstance(it, int) or it > 0 else min(E * REG, E * P * G * (g // G + 1))
                    pool.indirect_dma_start(
                        out=rowbuf[0:limit], out_offset=bass.IndirectOffsetOnAxis(ap=idx[:, i:i + 1], axis=0),
                        in_=rows[:, r, :], in_offset=None, bounds_check=limit - 1, oob_is_err=False,
                    ).then_inc(d_scat[r // G], 16)
                    pool.tensor_scalar(od[:, i, :], rows[:, r, 0:D], oa[:, b2, g % G:g % G + 1],
                                       oc[:, b2, g % G:g % G + 1], ALU.mult, ALU.add).then_inc(s_odw, 1)

                if isinstance(it, int) and it == 0 and k == BODY - 1:
                    pool.wait_ge(d_fill[2], 16 * (TPE - 2 * G))

            phase_a(pool, slot_fn, -LEAD_X0, LAG_OUT)

            for par in range(2):
                pool.wait_ge(d_out[par], 16 * (B // G // 2))

            def send(u, i):
                pool.wait_ge(b_fin, u * TB + i + 1)
                alone(pool)
                pool.indirect_dma_start(
                    out=out.rearrange("g n d -> (g n) d"),
                    out_offset=bass.IndirectOffsetOnAxis(ap=tok[:, i % RY:i % RY + 1], axis=0),
                    in_=yo[:, i % RY, :], in_offset=None, bounds_check=TOK - 1, oob_is_err=False,
                ).then_inc(b_sc[i % RY], 16)

            phase_b(pool, send)

        @block.scalar
        def _(act):
            act.wait_ge(s_fill, 1)
            act.wait_ge(d_w, 16 * (3 * KT + 6 + 3))
            rbf = rowbuf.rearrange("(c p e) r -> c p e r", e=E, c=TPE)
            for c in range(TPE):
                act.dma_start(rbf[c], fill[:].rearrange("p (o r) -> p o r", o=1).to_broadcast([P, E, ROW])
                              ).then_inc(d_fill[min(c // G, 2)], 16)

            def slot_fn(it, k):
                g = k + LEAD_XT
                gx = k - LAG_XFT
                if valid(it, g):
                    act.wait_ge(s_x0t, it * BODY + g + 1)
                    act.copy(xth[:, g % 2, :], ps_xt[:, 0:D]).then_inc(s_x0h, 1)
                if valid(it, gx):
                    act.wait_ge(s_xft, it * BODY + gx + 1)
                    act.copy(xft[:], ps_xt[:, D:2 * D]).then_inc(s_xfe, 1)
                g = k - 1
                if valid(it, g):
                    act.wait_ge(s_tt, it * BODY + g + 1)
                    act.copy(tt[:, g % 2, :], ps_t[:, P:2 * P]).then_inc(s_tte, 1)
                    act.wait_ge(s_tz2, it * BODY + g + 1)
                    act.copy(z1[:, g % 2, :], ps_z12[g % 2][:, D:2 * D]).then_inc(s_z1, 1)
                g = k
                if valid(it, g):
                    act.wait_ge(s_st, it * BODY + g + 1)
                    ge(act, s_em, it * BODY + g - 1)
                    act.activation(e1[:, g % 2, :], ps_t[:, 0:P], ACT.Exp, bias=svs[:, g % 2, 1:2])
                    act.activation(e2[:, g % 2, :], ps_t[:, 0:P], ACT.Exp, bias=svs[:, g % 2, 2:3],
                                   scale=SLOPE).then_inc(s_e, 1)
                    act.wait_ge(s_z12, it * BODY + g + 1)
                    act.copy(z2[:, g % 2, :], ps_z12[g % 2][:, 0:D]).then_inc(s_z2, 1)
                g = k - LAG_X1
                if valid(it, g):
                    act.wait_ge(s_mv2, it * BODY + g + 1)
                    act.mul(nm2[:, g % BODY:g % BODY + 1], mv2[:, g % 2, 0:1], -1.0)
                    act.add(ve2[:, g % 2:g % 2 + 1], mv2[:, g % 2, 1:2], EPS).then_inc(s_ve2, 1)
                g = k + LEAD_STATS - G
                if g % G == 0 and valid(it, g):
                    q = g // G % 2
                    act.wait_ge(s_mv1, it * BODY + g + G)
                    act.mul(nm1[:, q, :], mv1[:, q * G:(q + 1) * G, 0], -1.0)
                    act.add(ve1[:, q, :], mv1[:, q * G:(q + 1) * G, 1], EPS).then_inc(s_ve1, 1)
                g = k - LAG_ROUTE
                if g % G == 0 and valid(it, g):
                    act.wait_ge(s_df, bat(it, g) + 1)
                    act.activation(ex[:], df[:], ACT.Exp).then_inc(s_ex, 1)
                if isinstance(it, int) and it == PASSES - 1:
                    for e in experts_at(k):
                        act.wait_ge(d_ew[e % EWR], 16 * (1 + e // EWR))
                        act.copy(ewh[:, e], ewr[:, e % EWR]).then_inc(s_ewh, 1)

            phase_a(act, slot_fn, -LEAD_STATS, LAG_OUT)

            def norm(u, i):
                if i % HALF == 0:
                    h = i % TB // HALF
                    act.wait_ge(d_row[h], u * 16 + 16 * (i // TB) + 16)
                ge(act, b_xt, u * TB + i - RB + 1)
                r = i % TB
                act.activation(x0[:, i % RB, :], rin[:, r, 0:D], ACT.Identity, bias=rin[:, r, NMR:NMR + 1],
                               scale=rin[:, r, RSTD:RSTD + 1]).then_inc(b_xf, 1)

            def high(u, i):
                act.wait_ge(b_xt, u * TB + i + 1)
                act.copy(xth[:, i % RB, :], ps_bx[i % RB][:, 0:D]).then_inc(b_hi, 1)

            for i in range(4):
                norm(0, i)
            for i in range(2):
                high(0, i)

            def tile(u, i):
                if ahead(u, i + 2):
                    high(u, i + 2)
                if ahead(u, i + 4):
                    norm(u, i + 4)

            phase_b(act, tile)

        @block.vector
        def _(dve):
            vc = [0]

            def link(ins):
                vc[0] += 1
                ins.then_inc(s_vc, 1)
                dve.wait_ge(s_vc, vc[0])

            dve.wait_ge(d_w, 16 * (3 * KT + 6 + 3))
            link(dve.tensor_tensor(bks[:, 0, :], bkr[:, 0, :], bkr[:, 1, :], ALU.add))
            link(dve.tensor_tensor(bks[:, 1, :], bks[:, 0, :], bkr[:, 2, :], ALU.add))
            link(dve.tensor_copy(bkh[:], bks[:, 1, :]))
            link(dve.tensor_tensor(bkl[:], bks[:, 1, :], bkh[:].bitcast(F32), ALU.subtract))
            link(dve.tensor_copy(ebh[:], ebr[:]))
            link(dve.tensor_tensor(ebl[:], ebr[:], ebh[:].bitcast(F32), ALU.subtract))
            dve.wait_ge(s_pc, 11)
            link(dve.tensor_scalar(bvb[:, 0, :], onesf[:], bvt[:, 0:1], None, ALU.mult))
            link(dve.tensor_scalar(bvb[:, 1, :], onesf[:], bvt[:, 1:2], None, ALU.mult))
            dve.wait_ge(s_pe0, 1)
            for kt in range(KT):
                link(dve.tensor_copy(w0r[:, kt, D:D + 2], ps_set[:, 2 * kt:2 * kt + 2]))
                link(dve.tensor_scalar(w0r[:, kt, D + 2:D + 3], w0r[:, kt, D + 1:D + 2], SLOPE, None, ALU.mult))
            link(dve.tensor_copy(cjs[:], ps_set[:, 2 * KT:2 * KT + 2]))
            link(dve.tensor_tensor(csum[:, 0:1], cjs[:, 0:1], cjs[:, 1:2], ALU.add))
            link(dve.tensor_tensor(cvec[:, 1:2], csum[:, 0:1], abt[:], ALU.add))
            link(dve.tensor_scalar(cvec[:, 2:3], cvec[:, 1:2], SLOPE, None, ALU.mult))
            link(dve.tensor_copy(w12h[:], w12r[:]))
            link(dve.tensor_tensor(w12l[:], w12r[:], w12h[:].bitcast(F32), ALU.subtract))
            link(dve.tensor_copy(w0h[:], w0r[:]))
            link(dve.tensor_tensor(w0l[:], w0r[:], w0h[:].bitcast(F32), ALU.subtract))

            def slot_fn(it, k):
                def n(rel):
                    return it * BODY + rel + 1

                gr = k - LAG_ROUTE
                gp = gr - 1
                routes = gr % G == 0 and valid(it, gr)
                places = gp % G == 0 and valid(it, gp)

                g = k - LAG_X1
                if valid(it, g):
                    r = g % BODY
                    dve.wait_ge(s_tz1, n(g))
                    if g % G == 0:
                        ge(dve, d_scat[r // G], it * 16 * G + 16 * G * (g // BODY))
                    dve.scalar_tensor_tensor(rows[:, r, 0:D], ps_z0[g % 2][:, 0:D], 0.0, xin[:, r, :],
                                             ALU.max, ALU.add).then_inc(s_x1, 1)
                if routes:
                    add_bias(it, gr)
                if places:
                    sum_probs(it, gp)
                g = k + LEAD_XT
                if valid(it, g):
                    dve.wait_ge(s_x0h, n(g))
                    if valid(it, k - LAG_XFT):
                        dve.wait_ge(s_xfe, n(k - LAG_XFT))
                    dve.tensor_tensor(xtl[:, g % 2, :], ps_xt[:, 0:D], xth[:, g % 2, :].bitcast(F32),
                                      ALU.subtract).then_inc(s_x0l, 1)
                if routes:
                    top_logit(it, gr)
                if places:
                    probability(it, gp)
                g = k - LAG_X1
                if valid(it, g):
                    dve.wait_ge(s_x1, n(g))
                    dve.bn_stats(st2[:, g % 2, :], rows[:, g % BODY, 0:D]).then_inc(s_st2, 1)
                if routes:
                    differences(it, gr)
                g = k
                if valid(it, g):
                    dve.wait_ge(s_z0, n(g))
                    dve.tensor_tensor(svs[:, g % 2, :], ps_z0[g % 2][:, D:W0C], cvec[:], ALU.add).then_inc(s_sv, 1)
                g = k - LAG_X1
                if valid(it, g):
                    dve.wait_ge(s_st2, n(g))
                    alone(dve)
                    dve.bn_aggr(mv2[:, g % 2, :], st2[:, g % 2, :]).then_inc(s_mv2, 1)
                g = k + LEAD_STATS - 1
                if valid(it, g):
                    dve.wait_ge(s_st1, n(g))
                    alone(dve)
                    dve.bn_aggr(mv1[:, g % (2 * G), :], st1[:, g % 2, :]).then_inc(s_mv1, 1)
                if routes:
                    candidates(it, gr)
                g = k + LEAD_STATS
                if valid(it, g):
                    if g % G == 0:
                        dve.wait_ge(d_x[g % BODY // G], 32 * it + 32 * (g // BODY) + 32)
                    dve.bn_stats(st1[:, g % 2, :], xin[:, g % BODY, :]).then_inc(s_st1, 1)
                if routes:
                    first_candidate(it, gr)
                g = k
                c = g % 2
                if valid(it, g):
                    dve.wait_ge(s_e, n(g))
                    dve.tensor_tensor(em[:, c, :], e1[:, c, :], e2[:, c, :], ALU.max).then_inc(s_em, 1)
                if routes:
                    one_hot(it, gr)
                if places:
                    positions(it, gp)
                if valid(it, g):
                    dve.wait_ge(s_em, n(g))
                    dve.tensor_tensor_reduce(al[:, c, :], ain[:, g % BODY, :], em[:, c, :], 1.0, ROW_EPS,
                                             ALU.mult, ALU.add, rs[:, c:c + 1]).then_inc(s_al, 1)
                if places:
                    own_positions(it, gp)
                if valid(it, g):
                    dve.wait_ge(s_al, n(g))
                    dve.reciprocal(ri[:, c:c + 1], rs[:, c:c + 1]).then_inc(s_ri, 1)
                if places:
                    own_rows(it, gp)
                if valid(it, g):
                    dve.wait_ge(s_ri, n(g))
                    dve.tensor_scalar(tm[:, c, :], al[:, c, :], ri[:, c:c + 1], None, ALU.mult).then_inc(s_tm, 1)
                if places:
                    row_fields(it, gp)
                if isinstance(it, int) and it == PASSES - 1:
                    for e in experts_at(k):
                        dve.wait_ge(s_ewh, e + 1)
                        dve.tensor_tensor(ewl[:, e], ewr[:, e % EWR], ewh[:, e].bitcast(F32),
                                          ALU.subtract).then_inc(s_ewl, 1)

            NRO = 11

            def over_experts(v):
                return v.rearrange("p (g o) -> p g o", o=1).to_broadcast([P, G, E])

            def per_expert(v):
                return v.rearrange("p (g e) -> p g e", e=E)

            def add_bias(it, g):
                b = bat(it, g)
                dve.wait_ge(s_log, b + 1)
                dve.tensor_tensor(lg[:], per_expert(ps_lg[g // G % 2][:, 0:G * E]),
                                  swb[:].rearrange("p (o e) -> p o e", o=1).to_broadcast([P, G, E]),
                                  ALU.add).then_inc(s_lgr, 1)

            def top_logit(it, g):
                dve.wait_ge(s_lgr, bat(it, g) + 1)
                dve.tensor_reduce(mx[:], lg[:], AX_X, ALU.max).then_inc(s_ro, 1)

            def differences(it, g):
                dve.wait_ge(s_ro, bat(it, g) * NRO + 1)
                dve.tensor_tensor(df[:], lg[:], over_experts(mx[:]), ALU.subtract).then_inc(s_df, 1)

            def candidates(it, g):
                dve.wait_ge(s_df, bat(it, g) + 1)
                dve.scalar_tensor_tensor(wr[:], df[:], 0.0, rev[:], ALU.is_equal, ALU.mult).then_inc(s_ro, 1)

            def first_candidate(it, g):
                dve.wait_ge(s_ro, bat(it, g) * NRO + 2)
                dve.tensor_reduce(mr[:], wr[:], AX_X, ALU.max).then_inc(s_ro, 1)

            def one_hot(it, g):
                dve.wait_ge(s_ro, bat(it, g) * NRO + 3)
                dve.tensor_tensor(oh[:, g // G % 2], rev[:], over_experts(mr[:]), ALU.is_equal).then_inc(s_oh, 1)

            def sum_probs(it, g):
                dve.wait_ge(s_ex, bat(it, g) + 1)
                dve.tensor_reduce(sx[:], ex[:], AX_X, ALU.add).then_inc(s_ro, 1)

            def probability(it, g):
                r = g % BODY
                dve.wait_ge(s_ro, bat(it, g) * NRO + 4)
                dve.reciprocal(rows[:, r:r + G, PROB], sx[:]).then_inc(s_ro, 1)

            def positions(it, g):
                b2 = g // G % 2
                dve.wait_ge(s_pre, bat(it, g) + 1)
                if not isinstance(it, int) or g + it * BODY > 0:
                    dve.wait_ge(s_pos, bat(it, g))
                dve.tensor_tensor(
                    per_expert(pos[:, b2, :]), per_expert(ps_t[:, 2 * P:2 * P + (G + 1) * E]),
                    pos[:, 1 - b2, G * E:(G + 1) * E].rearrange("p (o e) -> p o e", o=1)
                    .to_broadcast([P, G + 1, E]), ALU.add).then_inc(s_pos, 1)

            def own_positions(it, g):
                b2 = g // G % 2
                dve.wait_ge(s_pos, bat(it, g) + 1)
                dve.wait_ge(s_oh, bat(it, g) + 1)
                dve.tensor_tensor(sel[:], oh[:, b2], per_expert(pos[:, b2, 0:G * E]), ALU.mult).then_inc(s_ro, 1)

            def own_rows(it, g):
                dve.wait_ge(s_ro, bat(it, g) * NRO + 6)
                dve.tensor_reduce(slot[:], sel[:], AX_X, ALU.add).then_inc(s_ro, 1)

            def row_fields(it, g):
                b = bat(it, g)
                b2 = g // G % 2
                r = g % BODY
                f = rows[:, r:r + G, :]
                dve.wait_ge(s_r2, it * BODY + g + G)
                dve.tensor_tensor(f[:, :, NMR], nm2[:, r:r + G], f[:, :, RSTD], ALU.mult).then_inc(s_ro, 1)
                dve.wait_ge(s_ro, b * NRO + 7)
                dve.tensor_scalar(far[:], slot[:], float(E * CAP), NOWHERE, ALU.is_ge, ALU.mult).then_inc(s_ro, 1)
                dve.tensor_tensor(pr[:], f[:, :, PROB], f[:, :, RSTD], ALU.mult).then_inc(s_ro, 1)
                ge(dve, s_odw, it * BODY + g - G)
                dve.wait_ge(s_ro, b * NRO + 8)
                dve.tensor_tensor(oc[:, b2, :], f[:, :, PROB], f[:, :, NMR], ALU.mult).then_inc(s_ro, 1)
                dve.wait_ge(s_ro, b * NRO + 10)
                dve.tensor_scalar(oa[:, b2, :], pr[:], 1.0, None, ALU.add)
                ge(dve, d_scat[(r // G - 2) % NB], it * 16 * G + 16 * G * ((g // G - 2) // NB + 1))
                dve.scalar_tensor_tensor(idx[:, b2 * G:(b2 + 1) * G], far[:], 1.0, slot[:], ALU.mult,
                                         ALU.add).then_inc(s_slot, 1)

            phase_a(dve, slot_fn, -LEAD_STATS, LAG_OUT)

            def low(u, i):
                dve.wait_ge(b_hi, u * TB + i + 1)
                dve.tensor_tensor(xtl[:, i % RB, :], ps_bx[i % RB][:, 0:D], xth[:, i % RB, :].bitcast(F32),
                                  ALU.subtract).then_inc(b_lo, 1)

            def finish(u, i):
                c = i % RY
                dve.wait_ge(b_y, u * TB + i + 1)
                ge(dve, b_sc[c], u * (16 * TB // RY) + 16 * (i // RY))
                dve.tensor_copy(tok[:, c:c + 1], rin[:, i, TOKEN:ROW])
                dve.scalar_tensor_tensor(yo[:, c, :], ps_by[i % RB][:, 0:D], rin[:, i, PROB:PROB + 1],
                                         rin[:, i, 0:D], ALU.mult, ALU.add).then_inc(b_fin, 1)

            for par in range(2):
                dve.wait_ge(d_out[par], 16 * (B // G // 2))
            for i in range(2):
                low(0, i)

            def tile(u, i):
                if ahead(u, i + 2):
                    low(u, i + 2)
                finish(u, i)

            phase_b(dve, tile)

        @block.tensor
        def _(pe):
            pe.wait_ge(d_w, 16 * (3 * KT + 6 + 3))
            pe.wait_ge(s_vc, 8)
            for kt in range(KT):
                for t in range(KT):
                    pe.matmul(ps_set[:, 2 * kt:2 * kt + 2], wvt[:, t, kt * P:(kt + 1) * P], awt[:, :, t],
                              start=(t == 0), stop=(t == KT - 1))
            for t in range(KT):
                mm = pe.matmul(ps_set[:, 2 * KT:2 * KT + 2], bvb[:, t, :], awt[:, :, t],
                               start=(t == 0), stop=(t == KT - 1))
            mm.then_inc(s_pe0, 1)
            pe.wait_ge(d_small, 16 * (1 + 2 * E))
            pe.wait_ge(s_vc, 20)

            def product(psum_out, part, lhs_h, lhs_l, rhs_h, rhs_l, start=False, stop=False):
                return pe.matmul(psum_out, lhs_l if part == 2 else lhs_h, rhs_l if part == 1 else rhs_h,
                                 start=start, stop=stop, skip_group_check=True)

            PARTS = [(part, t) for part in range(3) for t in range(KT)]

            def slot_fn(it, k):
                def n(rel):
                    return it * BODY + rel + 1

                c = k % 2

                def times_w(psum_out, w_h, w_l, steps, stop):
                    for part, t in steps:
                        ts = slice(t * P, (t + 1) * P)
                        mm = product(psum_out, part, xth[:, c, ts], xtl[:, c, ts], w_h[:, t, :], w_l[:, t, :],
                                     start=(part == 0 and t == 0), stop=stop and (part, t) == PARTS[-1])
                    return mm

                gx = k - LAG_XFT
                g = k + LEAD_XT
                if valid(it, k):
                    pe.wait_ge(s_x0l, n(k))
                if valid(it, gx - 1):
                    pe.wait_ge(s_xfe, n(gx - 1))
                if valid(it, gx):
                    pe.wait_ge(s_xf, n(gx))
                    for t in range(KT):
                        mm = pe.transpose(ps_xt[:, D + t * P:D + (t + 1) * P], xf[:, gx % 2, t * P:(t + 1) * P],
                                          ident[:])
                    mm.then_inc(s_xft, 1)
                if valid(it, g):
                    pe.wait_ge(s_x0, n(g))
                    for t in range(KT):
                        mm = pe.transpose(ps_xt[:, t * P:(t + 1) * P], x0[:, g % 2, t * P:(t + 1) * P], ident[:])
                    mm.then_inc(s_x0t, 1)
                if valid(it, k):
                    if valid(it, k - 2):
                        pe.wait_ge(s_z1, n(k - 2))
                    times_w(ps_z12[c][:], w12h, w12l, PARTS[:3], False)
                g = k - 1
                d = g % 2
                if valid(it, g):
                    pe.wait_ge(s_tm, n(g))
                    gr = k - LAG_ROUTE - 2
                    if gr % G == 0 and valid(it, gr):
                        pe.wait_ge(s_pos, bat(it, gr) + 1)
                    pe.transpose(ps_t[:, P:2 * P], tm[:, d, :], ident[:]).then_inc(s_tt, 1)
                if valid(it, k):
                    if valid(it, k - 2):
                        pe.wait_ge(s_x1, n(k - 2))
                    times_w(ps_z0[c][:, 0:W0C], w0h, w0l, PARTS, True).then_inc(s_z0, 1)
                if valid(it, g):
                    pe.wait_ge(s_tte, n(g))
                    pe.wait_ge(s_z2, n(g))
                    pe.matmul(ps_z12[d][:, D:2 * D], tt[:, d, :], z2[:, d, :], start=False, stop=True,
                              skip_group_check=True).then_inc(s_tz2, 1)
                gr = k - LAG_ROUTE - 1
                if gr % G == 0 and valid(it, gr):
                    pe.wait_ge(s_oh, bat(it, gr) + 1)
                    if not valid(it, g):
                        pe.wait_ge(s_pos, bat(it, gr))
                    ohf = oh[:, gr // G % 2].rearrange("p g e -> p (g e)")
                    o = 2 * P
                    for sh in range(1, G + 1):
                        pe.matmul(ps_t[:, o + sh * E:o + (G + 1) * E], steps_bf[:], ohf[:, 0:(G + 1 - sh) * E],
                                  start=(sh == 1), stop=False, skip_group_check=True)
                    pe.matmul(ps_t[:, o:o + G * E], before_bf[:], ohf, start=False, stop=True,
                              skip_group_check=True).then_inc(s_pre, 1)
                if valid(it, k):
                    times_w(ps_z12[c][:], w12h, w12l, PARTS[3:4], False)
                    pe.wait_ge(s_sv, n(k))
                    pe.transpose(ps_t[:, 0:P], svs[:, c, 0:1].to_broadcast([P, P]), ident[:]).then_inc(s_st, 1)
                    times_w(ps_z12[c][:], w12h, w12l, PARTS[4:], True).then_inc(s_z12, 1)
                if valid(it, gx):
                    j = gx % G
                    b2 = gx // G % 2
                    pe.wait_ge(s_xfe, n(gx))
                    if j == 0:
                        ge(pe, s_lgr, bat(it, gx) - 1)
                    for t in range(KT):
                        mm = pe.matmul(ps_lg[b2][:, j * E:(j + 1) * E], xft[:, t * P:(t + 1) * P], sw[:, t, :],
                                       start=(t == 0), stop=(t == KT - 1), skip_group_check=True)
                    if j == G - 1:
                        mm.then_inc(s_log, 1)
                if valid(it, g):
                    pe.wait_ge(s_z1, n(g))
                    pe.matmul(ps_z0[d][:, 0:D], tt[:, d, :], z1[:, d, :], start=False, stop=False,
                              skip_group_check=True)
                    pe.matmul(ps_z0[d][:, 0:D], ones2[:], bkh[:], start=False, stop=True,
                              skip_group_check=True).then_inc(s_tz1, 1)

            phase_a(pe, slot_fn, -LEAD_XT, LAG_OUT)

            def turn(u, i):
                pe.wait_ge(b_xf, u * TB + i + 1)
                ge(pe, b_lo, u * TB + i - RB + 1)
                for t in range(KT):
                    mm = pe.transpose(ps_bx[i % RB][:, t * P:(t + 1) * P], x0[:, i % RB, t * P:(t + 1) * P],
                                      ident[:])
                mm.then_inc(b_xt, 1)

            ewh_f = ewh[:].rearrange("p e t f -> p (e t f)")
            ewl_f = ewl[:].rearrange("p e t f -> p (e t f)")

            def expert(u, i):
                pe.wait_ge(b_lo, u * TB + i + 1)
                ge(pe, b_fin, u * TB + i - RB + 1)
                c = i % RB
                e = u * 2 + i // TPE
                y = ps_by[c][:, 0:D]
                for part, t in PARTS:
                    ts = slice(t * P, (t + 1) * P)
                    w = bass.ds(e * (KT * D) + t * D, D)
                    product(y, part, xth[:, c, ts], xtl[:, c, ts], ewh_f[:, w], ewl_f[:, w],
                            start=(part == 0 and t == 0))
                pe.matmul(y, ones2[:], ebp[:, bass.ds(e * D, D)], start=False, stop=True,
                          skip_group_check=True).then_inc(b_y, 1)

            for i in range(3):
                turn(0, i)

            def tile(u, i):
                if ahead(u, i + 3):
                    turn(u, i + 3)
                expert(u, i)

            pe.wait_ge(s_ewl, E)
            phase_b(pe, tile)


def kernel(x, adj, L0_gnn_Wv, L0_gnn_bv, L0_gnn_aw, L0_gnn_ab, L0_gnn_Wk, L0_gnn_bk, L0_ffn_switch_w,
           L0_ffn_switch_b, L0_ffn_expert_w, L0_ffn_expert_b):
    import numpy as np
    import concourse.bacc as bacc
    from concourse import mybir
    from concourse.bass_utils import run_bass_kernel_spmd

    ins = {
        "x": x, "adj": adj, "WvT": np.transpose(L0_gnn_Wv), "bv": np.transpose(np.reshape(L0_gnn_bv, (-1, P))),
        "aw": np.transpose(np.reshape(L0_gnn_aw, (-1, P))), "ab": L0_gnn_ab,
        "Wk": L0_gnn_Wk, "bk": L0_gnn_bk, "swT": np.transpose(L0_ffn_switch_w), "sb": L0_ffn_switch_b,
        "ewT": np.transpose(L0_ffn_expert_w, (0, 2, 1)), "eb": L0_ffn_expert_b,
    }
    nc = bacc.Bacc("TRN2", target_bir_lowering=False, num_devices=1)
    arrays, args = {}, []
    for name, a in ins.items():
        a = np.ascontiguousarray(a)
        arrays[f"in_{name}"] = a
        args.append(nc.dram_tensor(f"in_{name}", a.shape, mybir.dt.from_np(a.dtype), kind="ExternalInput").ap())
    out = nc.dram_tensor("out_0", list(x.shape), mybir.dt.float32, kind="ExternalOutput").ap()
    graph_then_experts(nc, *args, out)
    r = run_bass_kernel_spmd(nc, [arrays], core_ids=[0])
    return r.results[0]["out_0"]
```

```python
from contextlib import ExitStack

import concourse.bass as bass
from concourse import mybir

P = 128
ALU = mybir.AluOpType
ACT = mybir.ActivationFunctionType
F32 = mybir.dt.float32
F32R = mybir.dt.float32r
BF16 = mybir.dt.bfloat16
U32 = mybir.dt.uint32
AX_X = mybir.AxisListType.X

EPS = 1e-5
ROW_EPS = 1e-12
SLOPE = 0.2
CAPACITY_FACTOR = 1.2
BODY = 16
G = 4
FILL_AT = [-1, 0, 2, 4, 7, 8, 9, 10, 11, 12]
NOWHERE = 1.0e6

LAG_X1 = 2
LAG_XFT = 4
LAG_ROUTE = 8
LAG_OUT = 11
LEAD_STATS = 7
LEAD_X0 = 2
LEAD_XT = 1


def graph_then_experts(nc, x, adj, WvT, bv, aw, ab, Wk, bk, swT, sb_, ewT, eb, out):
    B, N, D = x.shape
    KT = D // P
    E = swT.shape[1]
    TOK = B * N
    CAP = int(CAPACITY_FACTOR * TOK / E)
    TPE = -(-CAP // P)
    REG = TPE * P
    HALF = TPE // 2
    ROW = D + 4
    NMR, RSTD, PROB, TOKEN = D, D + 1, D + 2, D + 3
    NV = 4
    W0C = D + NV
    PASSES = B // BODY
    RB, RY = 4, 5
    EPP = E // PASSES
    NB = BODY // G
    assert N == P and TPE % 2 == 0 and Wk.shape[0] == 3 and B % BODY == 0 and E == 2 * PASSES and len(FILL_AT) == TPE

    rowbuf = nc.dram_tensor("rowbuf", [E * REG, ROW], F32, kind="Internal").ap()
    parts = nc.dram_tensor("parts", [2, E, D], F32R, kind="Internal").ap()

    with ExitStack() as ctx:
        def sb(name, shape, dt=F32):
            return ctx.enter_context(nc.sbuf_tensor(name, shape, dt))

        def psum(name):
            return ctx.enter_context(nc.psum_tensor(name, [P, 512], F32))

        def sem(name):
            return ctx.enter_context(nc.semaphore(name))

        ps_z0 = [psum("ps_z0a"), psum("ps_z0b")]
        ps_z12 = [psum("ps_z12a"), psum("ps_z12b")]
        ps_xt = psum("ps_xt")
        ps_t = psum("ps_t")
        ps_lg = [psum("ps_lga"), psum("ps_lgb")]
        ps_set = ps_lg[1]
        ps_bx = [*ps_z12, ps_xt, ps_t]
        ps_by = [*ps_z0, *ps_lg]

        ident = sb("ident", [P, P])
        onesf = sb("onesf", [P, P])
        steps_bf = sb("steps_bf", [P, P], BF16)
        before_bf = sb("before_bf", [P, P], BF16)
        ones2 = sb("ones2", [2, P], F32R)
        rev = sb("rev", [P, G, E])
        swb = sb("swb", [P, E])
        sw = sb("sw", [P, KT, E])
        wvt = sb("wvt", [P, KT, D])
        awt = sb("awt", [P, 2, KT])
        bvt = sb("bvt", [P, KT])
        bvb = sb("bvb", [P, KT, P])
        abt = sb("abt", [P, 1])
        cvec = sb("cvec", [P, NV])
        csum = sb("csum", [P, 2])
        cjs = sb("cjs", [P, 2])
        w12r = sb("w12r", [P, KT, 2 * D])
        w12h = sb("w12h", [P, KT, 2 * D], F32R)
        w12l = sb("w12l", [P, KT, 2 * D], F32R)
        w0r = sb("w0r", [P, KT, W0C])
        w0h = sb("w0h", [P, KT, W0C], F32R)
        w0l = sb("w0l", [P, KT, W0C], F32R)
        bkr = sb("bkr", [2, 3, D])
        bks = sb("bks", [2, 2, D])
        bkh = sb("bkh", [2, D], F32R)
        bkl = sb("bkl", [2, D], F32R)
        ebr = sb("ebr", [E, D])
        ebh = sb("ebh", [E, D], F32R)
        ebl = sb("ebl", [E, D], F32R)
        ebp = sb("ebp", [2, E * D], F32R)
        fill = sb("fill", [P, ROW])
        ewr = sb("ewr", [P, EPP, KT, D])
        ewh = sb("ewh", [P, E, KT, D], F32R)
        ewl = sb("ewl", [P, E, KT, D], F32R)


        xin = sb("xin", [P, BODY, D])
        ain = sb("ain", [P, BODY, N])
        rows = sb("rows", [P, 2 * TPE, ROW])
        od = sb("od", [P, 2 * G, D])
        st1 = sb("st1", [P, 2, 6])
        mv1 = sb("mv1", [P, 2 * G, 2])
        ve1 = sb("ve1", [P, 2, G])
        nm1 = sb("nm1", [P, 2, G])
        r1 = sb("r1", [P, 2, G])
        mhalf = sb("mhalf", [P, G])
        x0 = sb("x0", [P, RB, D])
        xth = sb("xth", [P, RB, D], F32R)
        xtl = sb("xtl", [P, RB, D], F32R)
        svs = sb("svs", [P, 2, NV])
        e1 = sb("e1", [P, 2, N])
        e2 = sb("e2", [P, 2, N])
        em = sb("em", [P, 2, N])
        al = sb("al", [P, 2, N])
        rs = sb("rs", [P, 2])
        ri = sb("ri", [P, 2])
        tm = sb("tm", [P, 2, N])
        tt = sb("tt", [P, 2, N])
        z2 = sb("z2", [P, 2, D])
        z1 = sb("z1", [P, 2, D])
        st2 = sb("st2", [P, 2, 6])
        mv2 = sb("mv2", [P, 2, 2])
        ve2 = sb("ve2", [P, 2])
        nm2 = sb("nm2", [P, BODY])
        xf = sb("xf", [P, 2, D])
        xft = sb("xft", [P, D])
        lg = sb("lg", [P, G, E])
        mx = sb("mx", [P, G])
        df = sb("df", [P, G, E])
        wr = sb("wr", [P, G, E])
        mr = sb("mr", [P, G])
        ex = sb("ex", [P, G, E])
        sx = sb("sx", [P, G])
        oh = sb("oh", [P, 2, G, E], BF16)
        pos = sb("pos", [P, 2, (G + 1) * E])
        sel = sb("sel", [P, G, E])
        slot = sb("slot", [P, G])
        far = sb("far", [P, G])
        idx = sb("idx", [P, 2 * G], U32)
        pr = sb("pr", [P, G])
        oa = sb("oa", [P, 2, G])
        oc = sb("oc", [P, 2, G])

        rin = rows
        yo = od[:, 0:RY, :]
        tok = sb("tok", [P, RY], U32)

        d_v = sem("d_v")
        d_w = sem("d_w")
        d_bkh = sem("d_bkh")
        d_eb = sem("d_eb")
        d_ebp = sem("d_ebp")
        s_eb = sem("s_eb")
        d_ew = [sem(f"d_ew{q}") for q in range(EPP)]
        d_x = [sem(f"d_x{q}") for q in range(NB)]
        d_a = [sem(f"d_a{q}") for q in range(NB)]
        d_fill = [sem(f"d_fill{c}") for c in range(TPE)]
        d_scat = [sem(f"d_scat{q}") for q in range(NB)]
        d_out = [sem(f"d_out{q}") for q in range(2)]
        s_fill = sem("s_fill")
        s_passed = sem("s_passed")
        s_pc = sem("s_pc")
        s_vc = sem("s_vc")
        s_wh = sem("s_wh")
        s_pe0 = sem("s_pe0")
        s_st1 = sem("s_st1")
        s_mv1 = sem("s_mv1")
        s_ve1 = sem("s_ve1")
        s_r1 = sem("s_r1")
        s_x0 = sem("s_x0")
        s_x0t = sem("s_x0t")
        s_x0h = sem("s_x0h")
        s_x0l = sem("s_x0l")
        s_z0 = sem("s_z0")
        s_sv = sem("s_sv")
        s_z12 = sem("s_z12")
        s_z2 = sem("s_z2")
        s_st = sem("s_st")
        s_e = sem("s_e")
        s_em = sem("s_em")
        s_al = sem("s_al")
        s_ri = sem("s_ri")
        s_tm = sem("s_tm")
        s_tt = sem("s_tt")
        s_tte = sem("s_tte")
        s_tz2 = sem("s_tz2")
        s_z1 = sem("s_z1")
        s_tz1 = sem("s_tz1")
        s_x1 = sem("s_x1")
        s_st2 = sem("s_st2")
        s_mv2 = sem("s_mv2")
        s_ve2 = sem("s_ve2")
        s_r2 = sem("s_r2")
        s_xf = sem("s_xf")
        s_xft = sem("s_xft")
        s_xfe = sem("s_xfe")
        s_log = sem("s_log")
        s_lgr = sem("s_lgr")
        s_ro = sem("s_ro")
        s_df = sem("s_df")
        s_ex = sem("s_ex")
        s_oh = sem("s_oh")
        s_pre = sem("s_pre")
        s_pos = sem("s_pos")
        s_slot = sem("s_slot")
        s_tok = sem("s_tok")
        s_odw = sem("s_odw")
        s_ewh = sem("s_ewh")
        s_ewl = sem("s_ewl")
        d_row = [sem(f"d_row{h}") for h in range(4)]
        b_xf = sem("b_xf")
        b_xt = sem("b_xt")
        b_hi = sem("b_hi")
        b_lo = sem("b_lo")
        b_y = sem("b_y")
        b_fin = sem("b_fin")
        b_sc = [sem(f"b_sc{r}") for r in range(RY)]

        RO1, RO2 = 4, 8
        block = ctx.enter_context(nc.Block())

        def phase_a(eng, slot_fn, first, last):
            def run(it, lo, hi):
                for k in range(lo, hi):
                    slot_fn(it, k)
            run(0, first, BODY)
            with eng.Fori(1, PASSES - 1) as it:
                run(it, 0, BODY)
            run(PASSES - 1, 0, BODY + last)

        def valid(it, rel):
            return not isinstance(it, int) or 0 <= it * BODY + rel < B

        def ge(eng, s, value):
            if not isinstance(value, int) or value > 0:
                eng.wait_ge(s, value)

        def alone(eng):
            eng.sem_inc(s_passed, 1)

        def bat(it, rel):
            return it * NB + rel // G

        TB = 2 * TPE
        LAST = E * TPE // TB - 1

        def phase_b(eng, tile):
            for i in range(TB):
                tile(0, i)
            with eng.Fori(1, LAST) as u:
                for i in range(TB):
                    tile(u, i)
            for i in range(TB):
                tile(LAST, i)

        def ahead(u, i):
            return not (isinstance(u, int) and u == LAST and i >= TB)

        ewh_f = ewh[:].rearrange("p e t f -> p (e t f)")
        ewl_f = ewl[:].rearrange("p e t f -> p (e t f)")
        ewr_f = ewr[:].rearrange("p e t f -> p (e t f)")
        EW = KT * D

        def piece_at(k):
            m, rest = divmod(k + 1, BODY // (EPP * KT))
            return m - 1 if rest == 0 and 0 < m <= EPP * KT else None

        def piece(w, it, m):
            return w[:, bass.ds((it * EPP * KT + m) * D, D)]

        @block.sync
        def _(sp):
            xd = x.rearrange("(c g) n d -> c n g d", g=G)
            ad = adj.rearrange("(c g) n m -> c n g m", g=G)
            outd = out.rearrange("(c g) n d -> c n g d", g=G)

            def load(c, q):
                sp.dma_start(xin[:, q * G:(q + 1) * G, :], xd[c]).then_inc(d_x[q], 16)
                sp.dma_start(ain[:, q * G:(q + 1) * G, :], ad[c]).then_inc(d_a[q], 16)

            def load_expert(it, j):
                if not isinstance(it, int) or it * EPP + j >= EPP:
                    sp.wait_ge(s_ewl, it * (EPP * KT) + (j + 1 - EPP) * KT)
                sp.dma_start(ewr[:, j], ewT[it * EPP + j].rearrange("(t p) f -> p t f", p=P)).then_inc(d_ew[j], 16)

            sp.dma_start(xin[:, 0:G, :], xd[0]).then_inc(d_x[0], 16)
            sp.dma_start(wvt[:], WvT.rearrange("(t p) d -> p t d", p=P)).then_inc(d_v, 16)
            sp.dma_start(awt[:], aw.rearrange("p (h t) -> p h t", h=2)).then_inc(d_v, 16)
            sp.dma_start(bvt[:], bv).then_inc(d_v, 16)
            sp.dma_start(abt[:], ab.rearrange("(a o) -> a o", a=1).to_broadcast([P, 1])).then_inc(d_v, 16)
            for r in range(2):
                sp.dma_start(bkr[r:r + 1, :, :], bk.rearrange("(a k) d -> a k d", a=1)).then_inc(d_w, 16)
            for kt in range(KT):
                ks = slice(kt * P, (kt + 1) * P)
                sp.dma_start(w12r[:, kt, 0:D], Wk[2, ks, :]).then_inc(d_w, 16)
                sp.dma_start(w12r[:, kt, D:2 * D], Wk[1, ks, :]).then_inc(d_w, 16)
                sp.dma_start(w0r[:, kt, 0:D], Wk[0, ks, :]).then_inc(d_w, 16)
            sp.dma_start(xin[:, G:2 * G, :], xd[1]).then_inc(d_x[1], 16)
            sp.dma_start(ain[:, 0:G, :], ad[0]).then_inc(d_a[0], 16)
            sp.dma_start(swb[:], sb_.rearrange("(a o) -> a o", a=1).to_broadcast([P, E])).then_inc(d_w, 16)
            sp.dma_start(sw[:], swT.rearrange("(t p) e -> p t e", p=P)).then_inc(d_w, 16)
            sp.dma_start(ain[:, G:2 * G, :], ad[1]).then_inc(d_a[1], 16)
            sp.dma_start(ebr[:], eb).then_inc(d_eb, 16)
            sp.wait_ge(s_vc, KT + 4)
            sp.dma_start(bkh[1:2, :].bitcast(F32), bkl[0:1, :].bitcast(F32)).then_inc(d_bkh, 16)
            load(2, 2)
            load_expert(0, 0)
            for q in range(3, NB):
                load(q, q)
            sp.wait_ge(s_eb, 2)
            sp.dma_start(parts[0].bitcast(F32), ebh[:].bitcast(F32)).then_inc(d_ebp, 16)
            sp.dma_start(parts[1].bitcast(F32), ebl[:].bitcast(F32)).then_inc(d_ebp, 16)
            sp.wait_ge(d_ebp, 32)
            sp.dma_start(ebp[:].bitcast(F32), parts.rearrange("r e d -> r (e d)").bitcast(F32)).then_inc(d_ebp, 16)

            def store(it, c, par):
                ge(sp, s_odw, it * BODY + (c + 1) * G)
                sp.dma_start(outd[it * NB + c], od[:, par * G:(par + 1) * G, :]).then_inc(d_out[par], 16)

            def one_pass(it, loads):
                for q in range(NB):
                    if q == 1:
                        load_expert(it, 1)
                    if q == NB - 1 and loads:
                        load_expert(it + 1, 0)
                    if loads:
                        ge(sp, s_x1, it * BODY + (q + 1) * G)
                        load(it * NB + (q + NB), q)
                    if valid(it, (q - 2) * G):
                        store(it, q - 2, q % 2)

            one_pass(0, True)
            with sp.Fori(1, PASSES - 1) as it:
                one_pass(it, True)
            one_pass(PASSES - 1, False)
            store(PASSES - 1, NB - 2, 0)
            store(PASSES - 1, NB - 1, 1)

            for q in range(NB):
                sp.wait_ge(d_scat[q], 16 * G * PASSES)
            rb = rowbuf.rearrange("(h p i e) r -> e h p i r", h=2, p=P, i=HALF)

            def load_rows(u, h):
                sp.dma_start(rin[:, h * HALF:(h + 1) * HALF, :], rb[u * 2 + h // 2, h % 2]).then_inc(d_row[h], 16)

            for h in range(4):
                load_rows(0, h)
            with sp.Fori(1, LAST + 1) as u:
                for h in range(4):
                    sp.wait_ge(b_fin, u * TB + (HALF * (h + 1) - TB))
                    load_rows(u, h)
            for par in range(2):
                sp.wait_ge(d_out[par], 16 * (B // G // 2))
            for r in range(RY):
                sp.wait_ge(b_sc[r], 16 * E * TPE // RY)

        @block.gpsimd
        def _(pool):
            pool.memset(fill[:], 0.0).then_inc(s_pc, 1)
            pool.wait_ge(s_pc, 1)
            pool.memset(fill[:, TOKEN:ROW], NOWHERE).then_inc(s_fill, 1)
            pool.memset(onesf[:], 1.0).then_inc(s_pc, 1)
            pool.memset(steps_bf[:], float(E)).then_inc(s_pc, 1)
            pool.memset(mhalf[:], -0.5).then_inc(s_pc, 1)
            pool.memset(cvec[:], 0.0).then_inc(s_pc, 1)
            pool.memset(w0r[:, :, D:W0C], 0.0).then_inc(s_pc, 1)
            pool.memset(ones2[:].bitcast(F32), 1.0).then_inc(s_pc, 1)
            pool.wait_ge(s_pc, 3)
            pool.affine_select(ident[:], onesf[:], pattern=[[1, P]], compare_op=ALU.is_equal, fill=0.0,
                               base=0, channel_multiplier=-1).then_inc(s_pc, 1)
            pool.affine_select(before_bf[:], steps_bf[:], pattern=[[1, P]], compare_op=ALU.is_gt, fill=0.0,
                               base=0, channel_multiplier=-1).then_inc(s_pc, 1)
            pool.iota(rev[:], pattern=[[0, G], [-1, E]], base=E, channel_multiplier=0,
                      allow_small_or_imprecise_dtypes=True).then_inc(s_pc, 1)
            pool.iota(pos[:, 1, G * E:(G + 1) * E], pattern=[[1, E]], base=0, channel_multiplier=0,
                      allow_small_or_imprecise_dtypes=True).then_inc(s_pc, 1)
            pool.iota(rows[:, 0:G, TOKEN], pattern=[[P, G]], base=0, channel_multiplier=1,
                      allow_small_or_imprecise_dtypes=True).then_inc(s_tok, 1)

            def slot_fn(it, k):
                g = k + LEAD_X0
                if valid(it, g):
                    q = g // G % 2
                    if g % G == 0:
                        pool.wait_ge(s_ve1, bat(it, g) + 1)
                        pool.tensor_tensor(r1[:, q, :], ve1[:, q, :], mhalf[:], ALU.pow).then_inc(s_r1, 1)
                        pool.wait_ge(s_r1, bat(it, g) + 1)
                    ge(pool, s_x0t, it * BODY + g - 1)
                    alone(pool)
                    pool.tensor_scalar(x0[:, g % 2, :], xin[:, g % BODY, :], nm1[:, q, g % G:g % G + 1],
                                       r1[:, q, g % G:g % G + 1], ALU.add, ALU.mult).then_inc(s_x0, 1)
                g = k - LAG_X1
                if valid(it, g):
                    r = g % BODY
                    pool.wait_ge(s_ve2, it * BODY + g + 1)
                    pool.tensor_tensor(rows[:, r, RSTD:RSTD + 1], ve2[:, g % 2:g % 2 + 1], mhalf[:, 0:1],
                                       ALU.pow).then_inc(s_r2, 1)
                    pool.wait_ge(s_r2, it * BODY + g + 1)
                    ge(pool, s_xft, it * BODY + g - 1)
                    alone(pool)
                    pool.tensor_scalar(xf[:, g % 2, :], rows[:, r, 0:D], nm2[:, r:r + 1],
                                       rows[:, r, RSTD:RSTD + 1], ALU.add, ALU.mult).then_inc(s_xf, 1)
                g = k - LAG_OUT
                if valid(it, g):
                    r = g % BODY
                    b2 = g // G % 2
                    i = b2 * G + g % G
                    if g % G == 0:
                        pool.wait_ge(s_slot, bat(it, g) + 1)
                        pool.wait_ge(s_tok, bat(it, g) + 1)
                        alone(pool)
                    limit = E * REG
                    if isinstance(it, int) and it == 0:
                        limit = E * P * (g + 1)
                        pool.wait_ge(d_fill[g], 16)
                        alone(pool)
                    pool.indirect_dma_start(
                        out=rowbuf[0:limit], out_offset=bass.IndirectOffsetOnAxis(ap=idx[:, i:i + 1], axis=0),
                        in_=rows[:, r, :], in_offset=None, bounds_check=limit - 1, oob_is_err=False,
                    ).then_inc(d_scat[r // G], 16)
                    if g % G == G - 1 and valid(it, g + 1):
                        rp = r + 1 - G
                        rn = (r + 1) % BODY
                        pool.tensor_scalar(rows[:, rn:rn + G, TOKEN], rows[:, rp:rp + G, TOKEN],
                                           float(G * P), None, ALU.add).then_inc(s_tok, 1)
                if isinstance(it, int) and it == 0 and k == BODY - 1:
                    for c in range(BODY - LAG_OUT, TPE):
                        pool.wait_ge(d_fill[c], 16)

            pool.wait_ge(s_pc, 11)
            phase_a(pool, slot_fn, -LEAD_X0, LAG_OUT)

            for par in range(2):
                pool.wait_ge(d_out[par], 16 * (B // G // 2))

            def send(u, i):
                pool.wait_ge(b_fin, u * TB + i + 1)
                alone(pool)
                pool.indirect_dma_start(
                    out=out.rearrange("g n d -> (g n) d"),
                    out_offset=bass.IndirectOffsetOnAxis(ap=tok[:, i % RY:i % RY + 1], axis=0),
                    in_=yo[:, i % RY, :], in_offset=None, bounds_check=TOK - 1, oob_is_err=False,
                ).then_inc(b_sc[i % RY], 16)

            phase_b(pool, send)

        @block.scalar
        def _(act):
            act.wait_ge(s_fill, 1)
            rbf = rowbuf.rearrange("(c p e) r -> c p e r", e=E, c=TPE)

            act.wait_ge(d_w, 16 * (3 * KT + 4))
            act.copy(w12h[:], w12r[:]).then_inc(s_wh, 1)

            def fill_block(c):
                act.dma_start(rbf[c], fill[:].rearrange("p (o r) -> p o r", o=1).to_broadcast([P, E, ROW])
                              ).then_inc(d_fill[c], 16)

            def slot_fn(it, k):
                g = k + LEAD_XT
                gx = k - LAG_XFT
                if isinstance(it, int) and it == 0:
                    for c in range(TPE):
                        if k == FILL_AT[c]:
                            fill_block(c)
                if valid(it, g):
                    act.wait_ge(s_x0t, it * BODY + g + 1)
                    act.copy(xth[:, g % 2, :], ps_xt[:, 0:D]).then_inc(s_x0h, 1)
                if valid(it, gx):
                    act.wait_ge(s_xft, it * BODY + gx + 1)
                    act.copy(xft[:], ps_xt[:, D:2 * D]).then_inc(s_xfe, 1)
                g = k - 1
                if valid(it, g):
                    act.wait_ge(s_tt, it * BODY + g + 1)
                    act.copy(tt[:, g % 2, :], ps_t[:, P:2 * P]).then_inc(s_tte, 1)
                go = k - LAG_OUT
                if valid(it, go):
                    b2 = go // G % 2
                    j = go % G
                    if j == 0:
                        act.wait_ge(s_slot, bat(it, go) + 1)
                        ge(act, d_out[b2], 16 * 2 * it + 16 * ((go // G - b2) // 2))
                    act.activation(od[:, b2 * G + j, :], rows[:, go % BODY, 0:D], ACT.Identity,
                                   bias=oc[:, b2, j:j + 1], scale=oa[:, b2, j:j + 1]).then_inc(s_odw, 1)
                if valid(it, g):
                    act.wait_ge(s_tz2, it * BODY + g + 1)
                    act.copy(z1[:, g % 2, :], ps_z12[g % 2][:, D:2 * D]).then_inc(s_z1, 1)
                g = k
                if valid(it, g):
                    act.wait_ge(s_st, it * BODY + g + 1)
                    ge(act, s_em, it * BODY + g - 1)
                    act.activation(e1[:, g % 2, :], ps_t[:, 0:P], ACT.Exp, bias=svs[:, g % 2, 1:2])
                    act.activation(e2[:, g % 2, :], ps_t[:, 0:P], ACT.Exp, bias=svs[:, g % 2, 2:3],
                                   scale=SLOPE).then_inc(s_e, 1)
                    act.wait_ge(s_z12, it * BODY + g + 1)
                    act.copy(z2[:, g % 2, :], ps_z12[g % 2][:, 0:D]).then_inc(s_z2, 1)
                g = k - LAG_X1
                if valid(it, g):
                    act.wait_ge(s_mv2, it * BODY + g + 1)
                    act.mul(nm2[:, g % BODY:g % BODY + 1], mv2[:, g % 2, 0:1], -1.0)
                    act.add(ve2[:, g % 2:g % 2 + 1], mv2[:, g % 2, 1:2], EPS).then_inc(s_ve2, 1)
                g = k + LEAD_STATS - G
                if g % G == 0 and valid(it, g):
                    q = g // G % 2
                    act.wait_ge(s_mv1, it * BODY + g + G)
                    act.mul(nm1[:, q, :], mv1[:, q * G:(q + 1) * G, 0], -1.0)
                    act.add(ve1[:, q, :], mv1[:, q * G:(q + 1) * G, 1], EPS).then_inc(s_ve1, 1)
                g = k - LAG_ROUTE
                if g % G == 0 and valid(it, g):
                    act.wait_ge(s_df, bat(it, g) + 1)
                    act.activation(ex[:], df[:], ACT.Exp).then_inc(s_ex, 1)
                m = piece_at(k + 1)
                if m is not None:
                    act.wait_ge(d_ew[m // KT], it * 16 + 16)
                    act.copy(piece(ewh_f, it, m), ewr_f[:, m * D:(m + 1) * D]).then_inc(s_ewh, 1)

            phase_a(act, slot_fn, -LEAD_STATS, LAG_OUT)

            def norm(u, i):
                if i % HALF == 0:
                    h = i % TB // HALF
                    act.wait_ge(d_row[h], u * 16 + 16 * (i // TB) + 16)
                ge(act, b_xt, u * TB + i - RB + 1)
                r = i % TB
                act.activation(x0[:, i % RB, :], rin[:, r, 0:D], ACT.Identity, bias=rin[:, r, NMR:NMR + 1],
                               scale=rin[:, r, RSTD:RSTD + 1]).then_inc(b_xf, 1)

            def high(u, i):
                act.wait_ge(b_xt, u * TB + i + 1)
                act.copy(xth[:, i % RB, :], ps_bx[i % RB][:, 0:D]).then_inc(b_hi, 1)

            for i in range(4):
                norm(0, i)
            for i in range(2):
                high(0, i)

            def tile(u, i):
                if ahead(u, i + 2):
                    high(u, i + 2)
                if ahead(u, i + 4):
                    norm(u, i + 4)

            phase_b(act, tile)

        @block.vector
        def _(dve):
            vc = [0]

            def link(ins):
                vc[0] += 1
                ins.then_inc(s_vc, 1)
                dve.wait_ge(s_vc, vc[0])

            def set_up():
                dve.wait_ge(d_w, 16 * (3 * KT + 4))
                link(dve.tensor_tensor(bks[:, 0, :], bkr[:, 0, :], bkr[:, 1, :], ALU.add))
                link(dve.tensor_tensor(bks[:, 1, :], bks[:, 0, :], bkr[:, 2, :], ALU.add))
                link(dve.tensor_copy(bkh[:], bks[:, 1, :]))
                link(dve.tensor_tensor(bkl[:], bks[:, 1, :], bkh[:].bitcast(F32), ALU.subtract))
                dve.wait_ge(s_wh, 1)
                link(dve.tensor_tensor(w12l[:], w12r[:], w12h[:].bitcast(F32), ALU.subtract))
                dve.wait_ge(s_pe0, 1)
                for kt in range(KT):
                    dve.tensor_copy(w0r[:, kt, D:D + 2], ps_set[:, 2 * kt:2 * kt + 2])
                link(dve.tensor_copy(cjs[:], ps_set[:, 2 * KT:2 * KT + 2]))
                link(dve.tensor_scalar(w0r[:, :, D + 2], w0r[:, :, D + 1], SLOPE, None, ALU.mult))
                link(dve.tensor_copy(w0h[:], w0r[:]))
                link(dve.tensor_tensor(w0l[:], w0r[:], w0h[:].bitcast(F32), ALU.subtract))
                link(dve.tensor_tensor(csum[:, 0:1], cjs[:, 0:1], cjs[:, 1:2], ALU.add))
                link(dve.tensor_tensor(cvec[:, 1:2], csum[:, 0:1], abt[:], ALU.add))
                link(dve.tensor_scalar(cvec[:, 2:3], cvec[:, 1:2], SLOPE, None, ALU.mult))

            def expert_biases(it, k):
                if isinstance(it, int) and it == 0 and k == 0:
                    dve.wait_ge(d_eb, 16)
                    dve.tensor_copy(ebh[:], ebr[:]).then_inc(s_eb, 1)
                if isinstance(it, int) and it == 0 and k == 1:
                    dve.wait_ge(s_eb, 1)
                    dve.tensor_tensor(ebl[:], ebr[:], ebh[:].bitcast(F32), ALU.subtract).then_inc(s_eb, 1)

            def slot_fn(it, k):
                def n(rel):
                    return it * BODY + rel + 1

                gr = k - LAG_ROUTE
                gp = gr - 1
                routes = gr % G == 0 and valid(it, gr)
                places = gp % G == 0 and valid(it, gp)
                gf = gp - 1
                completes = gf % G == 0 and valid(it, gf)

                g = k - LAG_X1
                if valid(it, g):
                    r = g % BODY
                    dve.wait_ge(s_tz1, n(g))
                    if g % G == 0:
                        ge(dve, d_scat[r // G], it * 16 * G + 16 * G * (g // BODY))
                        ge(dve, s_odw, it * BODY + g - BODY + G)
                    dve.scalar_tensor_tensor(rows[:, r, 0:D], ps_z0[g % 2][:, 0:D], 0.0, xin[:, r, :],
                                             ALU.max, ALU.add).then_inc(s_x1, 1)
                if routes:
                    add_bias(it, gr)
                if places:
                    sum_probs(it, gp)
                if completes:
                    norm_field(it, gf)
                g = k + LEAD_XT
                if valid(it, g):
                    dve.wait_ge(s_x0h, n(g))
                    if valid(it, k - LAG_XFT):
                        dve.wait_ge(s_xfe, n(k - LAG_XFT))
                    dve.tensor_tensor(xtl[:, g % 2, :], ps_xt[:, 0:D], xth[:, g % 2, :].bitcast(F32),
                                      ALU.subtract).then_inc(s_x0l, 1)
                if routes:
                    top_logit(it, gr)
                if places:
                    probability(it, gp)
                if completes:
                    dropped(it, gf)
                g = k - LAG_X1
                if valid(it, g):
                    dve.wait_ge(s_x1, n(g))
                    dve.bn_stats(st2[:, g % 2, :], rows[:, g % BODY, 0:D]).then_inc(s_st2, 1)
                g = k
                if valid(it, g):
                    dve.wait_ge(s_z0, n(g))
                    dve.tensor_tensor(svs[:, g % 2, :], ps_z0[g % 2][:, D:W0C], cvec[:], ALU.add).then_inc(s_sv, 1)
                if routes:
                    differences(it, gr)
                if completes:
                    default_factors(it, gf)
                g = k - LAG_X1
                if valid(it, g):
                    dve.wait_ge(s_st2, n(g))
                    alone(dve)
                    dve.bn_aggr(mv2[:, g % 2, :], st2[:, g % 2, :]).then_inc(s_mv2, 1)
                g = k + LEAD_STATS - 1
                if valid(it, g):
                    dve.wait_ge(s_st1, n(g))
                    alone(dve)
                    dve.bn_aggr(mv1[:, g % (2 * G), :], st1[:, g % 2, :]).then_inc(s_mv1, 1)
                if routes:
                    candidates(it, gr)
                if completes:
                    row_of_token(it, gf)
                g = k + LEAD_STATS
                if valid(it, g):
                    if g % G == 0:
                        dve.wait_ge(d_x[g % BODY // G], 16 * it + 16 * (g // BODY) + 16)
                    dve.bn_stats(st1[:, g % 2, :], xin[:, g % BODY, :]).then_inc(s_st1, 1)
                m = piece_at(k)
                if m is not None:
                    dve.wait_ge(s_ewh, it * (EPP * KT) + m + 1)
                    dve.tensor_tensor(piece(ewl_f, it, m), ewr_f[:, m * D:(m + 1) * D],
                                      piece(ewh_f, it, m).bitcast(F32), ALU.subtract).then_inc(s_ewl, 1)
                if routes:
                    first_candidate(it, gr)
                g = k
                c = g % 2
                if valid(it, g):
                    dve.wait_ge(s_e, n(g))
                    dve.tensor_tensor(em[:, c, :], e1[:, c, :], e2[:, c, :], ALU.max).then_inc(s_em, 1)
                if routes:
                    one_hot(it, gr)
                if places:
                    positions(it, gp)
                if valid(it, g):
                    dve.wait_ge(s_em, n(g))
                    if g % G == 0:
                        dve.wait_ge(d_a[g // G], 16 * it + 16)
                    dve.tensor_tensor_reduce(al[:, c, :], ain[:, g % BODY, :], em[:, c, :], 1.0, ROW_EPS,
                                             ALU.mult, ALU.add, rs[:, c:c + 1]).then_inc(s_al, 1)
                if places:
                    own_positions(it, gp)
                if valid(it, g):
                    dve.wait_ge(s_al, n(g))
                    dve.reciprocal(ri[:, c:c + 1], rs[:, c:c + 1]).then_inc(s_ri, 1)
                if places:
                    own_rows(it, gp)
                if valid(it, g):
                    dve.wait_ge(s_ri, n(g))
                    dve.tensor_scalar(tm[:, c, :], al[:, c, :], ri[:, c:c + 1], None, ALU.mult).then_inc(s_tm, 1)
                expert_biases(it, k)
            NRO = 11

            def over_experts(v):
                return v.rearrange("p (g o) -> p g o", o=1).to_broadcast([P, G, E])

            def per_expert(v):
                return v.rearrange("p (g e) -> p g e", e=E)

            def add_bias(it, g):
                b = bat(it, g)
                dve.wait_ge(s_log, b + 1)
                dve.tensor_tensor(lg[:], per_expert(ps_lg[g // G % 2][:, 0:G * E]),
                                  swb[:].rearrange("p (o e) -> p o e", o=1).to_broadcast([P, G, E]),
                                  ALU.add).then_inc(s_lgr, 1)

            def top_logit(it, g):
                dve.wait_ge(s_lgr, bat(it, g) + 1)
                dve.tensor_reduce(mx[:], lg[:], AX_X, ALU.max).then_inc(s_ro, 1)

            def differences(it, g):
                dve.wait_ge(s_ro, bat(it, g) * NRO + 1)
                dve.tensor_tensor(df[:], lg[:], over_experts(mx[:]), ALU.subtract).then_inc(s_df, 1)

            def candidates(it, g):
                dve.wait_ge(s_df, bat(it, g) + 1)
                dve.scalar_tensor_tensor(wr[:], df[:], 0.0, rev[:], ALU.is_equal, ALU.mult).then_inc(s_ro, 1)

            def first_candidate(it, g):
                dve.wait_ge(s_ro, bat(it, g) * NRO + 2)
                dve.tensor_reduce(mr[:], wr[:], AX_X, ALU.max).then_inc(s_ro, 1)

            def one_hot(it, g):
                dve.wait_ge(s_ro, bat(it, g) * NRO + 3)
                dve.tensor_tensor(oh[:, g // G % 2], rev[:], over_experts(mr[:]), ALU.is_equal).then_inc(s_oh, 1)

            def sum_probs(it, g):
                dve.wait_ge(s_ex, bat(it, g) + 1)
                dve.tensor_reduce(sx[:], ex[:], AX_X, ALU.add).then_inc(s_ro, 1)

            def probability(it, g):
                r = g % BODY
                dve.wait_ge(s_ro, bat(it, g) * NRO + 4)
                dve.reciprocal(rows[:, r:r + G, PROB], sx[:]).then_inc(s_ro, 1)

            def positions(it, g):
                b2 = g // G % 2
                dve.wait_ge(s_pre, bat(it, g) + 1)
                if not isinstance(it, int) or g + it * BODY > 0:
                    dve.wait_ge(s_pos, bat(it, g))
                dve.tensor_tensor(
                    per_expert(pos[:, b2, :]), per_expert(ps_t[:, 2 * P:2 * P + (G + 1) * E]),
                    pos[:, 1 - b2, G * E:(G + 1) * E].rearrange("p (o e) -> p o e", o=1)
                    .to_broadcast([P, G + 1, E]), ALU.add).then_inc(s_pos, 1)

            def own_positions(it, g):
                b2 = g // G % 2
                dve.wait_ge(s_pos, bat(it, g) + 1)
                dve.wait_ge(s_oh, bat(it, g) + 1)
                dve.tensor_tensor(sel[:], oh[:, b2], per_expert(pos[:, b2, 0:G * E]), ALU.mult).then_inc(s_ro, 1)

            def own_rows(it, g):
                dve.wait_ge(s_ro, bat(it, g) * NRO + 6)
                dve.tensor_reduce(slot[:], sel[:], AX_X, ALU.add).then_inc(s_ro, 1)

            def fields(it, g):
                r = g % BODY
                return bat(it, g), g // G % 2, r, rows[:, r:r + G, :]

            def norm_field(it, g):
                b, b2, r, f = fields(it, g)
                dve.wait_ge(s_r2, it * BODY + g + G)
                dve.tensor_tensor(f[:, :, NMR], nm2[:, r:r + G], f[:, :, RSTD], ALU.mult).then_inc(s_ro, 1)

            def dropped(it, g):
                b, b2, r, f = fields(it, g)
                dve.wait_ge(s_ro, b * NRO + 7)
                dve.tensor_scalar(far[:], slot[:], float(E * CAP), NOWHERE, ALU.is_ge, ALU.mult).then_inc(s_ro, 1)
                dve.tensor_tensor(pr[:], f[:, :, PROB], f[:, :, RSTD], ALU.mult).then_inc(s_ro, 1)

            def default_factors(it, g):
                b, b2, r, f = fields(it, g)
                ge(dve, s_odw, it * BODY + g - G)
                dve.wait_ge(s_ro, b * NRO + 8)
                dve.tensor_tensor(oc[:, b2, :], f[:, :, PROB], f[:, :, NMR], ALU.mult).then_inc(s_ro, 1)
                dve.wait_ge(s_ro, b * NRO + 10)
                dve.tensor_scalar(oa[:, b2, :], pr[:], 1.0, None, ALU.add)

            def row_of_token(it, g):
                b, b2, r, f = fields(it, g)
                ge(dve, d_scat[(r // G - 2) % NB], it * 16 * G + 16 * G * ((g // G - 2) // NB + 1))
                dve.scalar_tensor_tensor(idx[:, b2 * G:(b2 + 1) * G], far[:], 1.0, slot[:], ALU.mult,
                                         ALU.add).then_inc(s_slot, 1)

            dve.wait_ge(s_pc, 11)
            dve.wait_ge(d_v, 16 * 4)
            for t in range(KT):
                link(dve.tensor_scalar(bvb[:, t, :], onesf[:], bvt[:, t:t + 1], None, ALU.mult))
            for k in range(-LEAD_STATS, -LEAD_STATS + G + 1):
                slot_fn(0, k)
            set_up()
            phase_a(dve, slot_fn, -LEAD_STATS + G + 1, LAG_OUT)

            def low(u, i):
                dve.wait_ge(b_hi, u * TB + i + 1)
                dve.tensor_tensor(xtl[:, i % RB, :], ps_bx[i % RB][:, 0:D], xth[:, i % RB, :].bitcast(F32),
                                  ALU.subtract).then_inc(b_lo, 1)

            def finish(u, i):
                c = i % RY
                dve.wait_ge(b_y, u * TB + i + 1)
                ge(dve, b_sc[c], u * (16 * TB // RY) + 16 * (i // RY))
                dve.tensor_copy(tok[:, c:c + 1], rin[:, i, TOKEN:ROW])
                dve.scalar_tensor_tensor(yo[:, c, :], ps_by[i % RB][:, 0:D], rin[:, i, PROB:PROB + 1],
                                         rin[:, i, 0:D], ALU.mult, ALU.add).then_inc(b_fin, 1)

            for i in range(2):
                low(0, i)
            for par in range(2):
                dve.wait_ge(d_out[par], 16 * (B // G // 2))

            def tile(u, i):
                if ahead(u, i + 2):
                    low(u, i + 2)
                finish(u, i)

            phase_b(dve, tile)

        @block.tensor
        def _(pe):
            pe.wait_ge(d_v, 16 * 4)
            pe.wait_ge(s_vc, KT)
            for kt in range(KT):
                for t in range(KT):
                    pe.matmul(ps_set[:, 2 * kt:2 * kt + 2], wvt[:, t, kt * P:(kt + 1) * P], awt[:, :, t],
                              start=(t == 0), stop=(t == KT - 1))
            for t in range(KT):
                mm = pe.matmul(ps_set[:, 2 * KT:2 * KT + 2], bvb[:, t, :], awt[:, :, t],
                               start=(t == 0), stop=(t == KT - 1))
            mm.then_inc(s_pe0, 1)

            def product(psum_out, part, lhs_h, lhs_l, rhs_h, rhs_l, start=False, stop=False):
                return pe.matmul(psum_out, lhs_l if part == 2 else lhs_h, rhs_l if part == 1 else rhs_h,
                                 start=start, stop=stop, skip_group_check=True)

            PARTS = [(part, t) for part in range(3) for t in range(KT)]

            def slot_fn(it, k):
                def n(rel):
                    return it * BODY + rel + 1

                c = k % 2

                def times_w(psum_out, w_h, w_l, steps, stop):
                    for part, t in steps:
                        ts = slice(t * P, (t + 1) * P)
                        mm = product(psum_out, part, xth[:, c, ts], xtl[:, c, ts], w_h[:, t, :], w_l[:, t, :],
                                     start=(part == 0 and t == 0), stop=stop and (part, t) == PARTS[-1])
                    return mm

                gx = k - LAG_XFT
                g = k + LEAD_XT
                if valid(it, k):
                    pe.wait_ge(s_x0l, n(k))
                if valid(it, gx - 1):
                    pe.wait_ge(s_xfe, n(gx - 1))
                if valid(it, gx):
                    pe.wait_ge(s_xf, n(gx))
                    for t in range(KT):
                        mm = pe.transpose(ps_xt[:, D + t * P:D + (t + 1) * P], xf[:, gx % 2, t * P:(t + 1) * P],
                                          ident[:])
                    mm.then_inc(s_xft, 1)
                if valid(it, g):
                    pe.wait_ge(s_x0, n(g))
                    for t in range(KT):
                        mm = pe.transpose(ps_xt[:, t * P:(t + 1) * P], x0[:, g % 2, t * P:(t + 1) * P], ident[:])
                    mm.then_inc(s_x0t, 1)
                if valid(it, k):
                    if isinstance(it, int) and it * BODY + k == 0:
                        pe.wait_ge(d_w, 16 * (3 * KT + 4))
                        pe.wait_ge(s_vc, KT + 12)
                    if valid(it, k - 2):
                        pe.wait_ge(s_z1, n(k - 2))
                    times_w(ps_z12[c][:], w12h, w12l, PARTS[:3], False)
                g = k - 1
                d = g % 2
                if valid(it, g):
                    pe.wait_ge(s_tm, n(g))
                    gr = k - LAG_ROUTE - 2
                    if gr % G == 0 and valid(it, gr):
                        pe.wait_ge(s_pos, bat(it, gr) + 1)
                    pe.transpose(ps_t[:, P:2 * P], tm[:, d, :], ident[:]).then_inc(s_tt, 1)
                if valid(it, k):
                    if valid(it, k - 2):
                        pe.wait_ge(s_x1, n(k - 2))
                    times_w(ps_z0[c][:, 0:W0C], w0h, w0l, PARTS, True).then_inc(s_z0, 1)
                if valid(it, g):
                    pe.wait_ge(s_tte, n(g))
                    pe.wait_ge(s_z2, n(g))
                    pe.matmul(ps_z12[d][:, D:2 * D], tt[:, d, :], z2[:, d, :], start=False, stop=True,
                              skip_group_check=True).then_inc(s_tz2, 1)
                gr = k - LAG_ROUTE - 1
                if gr % G == 0 and valid(it, gr):
                    pe.wait_ge(s_oh, bat(it, gr) + 1)
                    if not valid(it, g):
                        pe.wait_ge(s_pos, bat(it, gr))
                    ohf = oh[:, gr // G % 2].rearrange("p g e -> p (g e)")
                    o = 2 * P
                    for sh in range(1, G + 1):
                        pe.matmul(ps_t[:, o + sh * E:o + (G + 1) * E], steps_bf[:], ohf[:, 0:(G + 1 - sh) * E],
                                  start=(sh == 1), stop=False, skip_group_check=True)
                    pe.matmul(ps_t[:, o:o + G * E], before_bf[:], ohf, start=False, stop=True,
                              skip_group_check=True).then_inc(s_pre, 1)
                if valid(it, k):
                    times_w(ps_z12[c][:], w12h, w12l, PARTS[3:4], False)
                    pe.wait_ge(s_sv, n(k))
                    pe.transpose(ps_t[:, 0:P], svs[:, c, 0:1].to_broadcast([P, P]), ident[:]).then_inc(s_st, 1)
                    times_w(ps_z12[c][:], w12h, w12l, PARTS[4:], True).then_inc(s_z12, 1)
                if valid(it, gx):
                    j = gx % G
                    b2 = gx // G % 2
                    pe.wait_ge(s_xfe, n(gx))
                    if j == 0:
                        ge(pe, s_lgr, bat(it, gx) - 1)
                    for t in range(KT):
                        mm = pe.matmul(ps_lg[b2][:, j * E:(j + 1) * E], xft[:, t * P:(t + 1) * P], sw[:, t, :],
                                       start=(t == 0), stop=(t == KT - 1), skip_group_check=True)
                    if j == G - 1:
                        mm.then_inc(s_log, 1)
                if valid(it, g):
                    pe.wait_ge(s_z1, n(g))
                    pe.matmul(ps_z0[d][:, 0:D], tt[:, d, :], z1[:, d, :], start=False, stop=False,
                              skip_group_check=True)
                    if isinstance(it, int) and it * BODY + g == 0:
                        pe.wait_ge(d_bkh, 16)
                    pe.matmul(ps_z0[d][:, 0:D], ones2[:], bkh[:], start=False, stop=True,
                              skip_group_check=True).then_inc(s_tz1, 1)

            phase_a(pe, slot_fn, -LEAD_XT, LAG_OUT)

            def turn(u, i):
                pe.wait_ge(b_xf, u * TB + i + 1)
                ge(pe, b_lo, u * TB + i - RB + 1)
                for t in range(KT):
                    mm = pe.transpose(ps_bx[i % RB][:, t * P:(t + 1) * P], x0[:, i % RB, t * P:(t + 1) * P],
                                      ident[:])
                mm.then_inc(b_xt, 1)

            def expert(u, i):
                pe.wait_ge(b_lo, u * TB + i + 1)
                ge(pe, b_fin, u * TB + i - RB + 1)
                c = i % RB
                e = u * 2 + i // TPE
                y = ps_by[c][:, 0:D]
                for part, t in PARTS:
                    ts = slice(t * P, (t + 1) * P)
                    w = bass.ds(e * EW + t * D, D)
                    product(y, part, xth[:, c, ts], xtl[:, c, ts], ewh_f[:, w], ewl_f[:, w],
                            start=(part == 0 and t == 0))
                pe.matmul(y, ones2[:], ebp[:, bass.ds(e * D, D)], start=False, stop=True,
                          skip_group_check=True).then_inc(b_y, 1)

            for i in range(3):
                turn(0, i)

            def tile(u, i):
                if ahead(u, i + 3):
                    turn(u, i + 3)
                expert(u, i)

            pe.wait_ge(d_ebp, 48)
            pe.wait_ge(s_ewl, E * KT)
            phase_b(pe, tile)


def kernel(x, adj, L0_gnn_Wv, L0_gnn_bv, L0_gnn_aw, L0_gnn_ab, L0_gnn_Wk, L0_gnn_bk, L0_ffn_switch_w,
           L0_ffn_switch_b, L0_ffn_expert_w, L0_ffn_expert_b):
    import numpy as np
    import concourse.bacc as bacc
    from concourse import mybir
    from concourse.bass_utils import run_bass_kernel_spmd

    ins = {
        "x": x, "adj": adj, "WvT": np.transpose(L0_gnn_Wv), "bv": np.transpose(np.reshape(L0_gnn_bv, (-1, P))),
        "aw": np.transpose(np.reshape(L0_gnn_aw, (-1, P))), "ab": L0_gnn_ab,
        "Wk": L0_gnn_Wk, "bk": L0_gnn_bk, "swT": np.transpose(L0_ffn_switch_w), "sb": L0_ffn_switch_b,
        "ewT": np.transpose(L0_ffn_expert_w, (0, 2, 1)), "eb": L0_ffn_expert_b,
    }
    nc = bacc.Bacc("TRN2", target_bir_lowering=False, num_devices=1)
    arrays, args = {}, []
    for name, a in ins.items():
        a = np.ascontiguousarray(a)
        arrays[f"in_{name}"] = a
        args.append(nc.dram_tensor(f"in_{name}", a.shape, mybir.dt.from_np(a.dtype), kind="ExternalInput").ap())
    out = nc.dram_tensor("out_0", list(x.shape), mybir.dt.float32, kind="ExternalOutput").ap()
    graph_then_experts(nc, *args, out)
    r = run_bass_kernel_spmd(nc, [arrays], core_ids=[0])
    return r.results[0]["out_0"]
```
